# Optimizing a Trainium2 kernel written in Bass

```python
import numpy as np
import jax
import jax.numpy as jnp

def _softmax(x, axis=-1):
    return jax.nn.softmax(x, axis=axis)

def _gelu(x):
    return jax.nn.gelu(x, approximate=True)

def _silu(x):
    return jax.nn.silu(x)

def _sigmoid(x):
    return jax.nn.sigmoid(x)

def _layernorm(x, axis=-1, eps=1e-05):
    m = jnp.mean(x, axis=axis, keepdims=True)
    v = jnp.var(x, axis=axis, keepdims=True)
    return (x - m) / jnp.sqrt(v + eps)

def _scatter_add(tgt, idx, src, axis=0):
    return tgt.at[idx].add(src)

def _segment_sum(src, seg, n):
    return jax.ops.segment_sum(src, seg, n)
kernel_name = 'mk_gnn_resnorm_d4_gnn_r8_eabedd'

def setup_inputs(seed: int=0):
    np.random.seed(seed)
    _w = jnp.asarray

    def _rec_inputs():
        import jax
        import jax.numpy as jnp
        _gk = jax.random.key(seed)
        x = -0.0005121 + 1.001 * jax.random.normal(jax.random.fold_in(_gk, 1), (6250, 64), jnp.float32)
        _s = jax.random.randint(jax.random.fold_in(_gk, 2), (100000,), 0, 6250, jnp.int32)
        _d = jax.random.randint(jax.random.fold_in(_gk, 3), (100000,), 0, 6250, jnp.int32)
        _loop = jnp.arange(6250, dtype=jnp.int32)
        src = jnp.concatenate([_s, _d, _loop])
        dst = jnp.concatenate([_d, _s, _loop])
        _o = jnp.argsort(dst, stable=True)
        src = src[_o]
        dst = dst[_o]
        edge_type_65 = jax.random.randint(jax.random.fold_in(_gk, 12), (206250,), 0, 65, jnp.int32)
        return (x, src, dst, edge_type_65)
    x, src, dst, edge_type_65 = _rec_inputs()

    def _L0_gnn_setup():
        import jax, jax.numpy as jnp
        import numpy as np
        N, E, D, R, L = (6250, 75000, 64, 65, 2)

        def _rgcn_conv(x, src, dst, edge_type, W_r, W_root, b):
            n, d = x.shape
            r = W_r.shape[0]
            seg = dst * r + edge_type
            msg = x[src]
            agg = jax.ops.segment_sum(msg, seg, num_segments=n * r).reshape(n, r, d)
            cnt = jax.ops.segment_sum(jnp.ones((msg.shape[0],), x.dtype), seg, num_segments=n * r).reshape(n, r, 1)
            mean = agg / jnp.maximum(cnt, 1.0)
            out = jnp.einsum('nrd,rdk->nk', mean, W_r)
            return out + x @ W_root + b
        key = jax.random.key(seed)
        ks = jax.random.split(key, 10)
        x = jax.random.normal(ks[0], (N, D), dtype=jnp.float32)
        edge_index = jax.random.randint(ks[1], (2, E), 0, N, dtype=jnp.int64)
        edge_type = jax.random.randint(ks[2], (E,), 0, R, dtype=jnp.int64)
        s = 1.0 / np.sqrt(D)
        W = jax.random.normal(ks[3], (L, R, D, D), dtype=jnp.float32) * s
        root = jax.random.normal(ks[4], (L, D, D), dtype=jnp.float32) * s
        bias = jax.random.normal(ks[5], (L, D), dtype=jnp.float32) * 0.01
        res_W = jax.random.normal(ks[6], (L, D, D), dtype=jnp.float32) * s
        res_b = jax.random.normal(ks[7], (L, D), dtype=jnp.float32) * 0.01
        return {'x': x, 'edge_index': edge_index, 'edge_type': edge_type, 'W': W, 'root': root, 'bias': bias, 'res_W': res_W, 'res_b': res_b}
    _L0_gnn_all = _L0_gnn_setup()
    _L0_gnn_in = {k: v for k, v in _L0_gnn_all.items() if k in ('W', 'root', 'bias', 'res_W', 'res_b')}
    del _L0_gnn_all

    def _L1_gnn_setup():
        import jax, jax.numpy as jnp
        import numpy as np
        N = 12500
        E = 200000
        IN_DIM = 64
        OUT_DIM = 64
        BN_EPS = 1e-05
        key = jax.random.key(seed)
        ks = jax.random.split(key, 5)
        x = jax.random.normal(ks[0], (N, IN_DIM), dtype=jnp.float32)
        edge_index = jax.random.randint(ks[1], (2, E), 0, N, dtype=jnp.int64)
        s1 = 1.0 / np.sqrt(IN_DIM)
        s2 = 1.0 / np.sqrt(OUT_DIM)
        W1 = jax.random.uniform(ks[2], (IN_DIM, OUT_DIM), jnp.float32, -s1, s1)
        W2 = jax.random.uniform(ks[3], (OUT_DIM, OUT_DIM), jnp.float32, -s2, s2)
        b1 = jnp.zeros((OUT_DIM,), jnp.float32)
        b2 = jnp.zeros((OUT_DIM,), jnp.float32)
        gamma = jnp.ones((OUT_DIM,), jnp.float32)
        beta = jnp.zeros((OUT_DIM,), jnp.float32)
        return {'x': x, 'edge_index': edge_index, 'W1': W1, 'b1': b1, 'W2': W2, 'b2': b2, 'gamma': gamma, 'beta': beta}
    _L1_gnn_all = _L1_gnn_setup()
    _L1_gnn_in = {k: v for k, v in _L1_gnn_all.items() if k in ('W1', 'b1', 'W2', 'b2', 'gamma', 'beta')}
    del _L1_gnn_all

    def _L2_gnn_setup():
        import jax, jax.numpy as jnp
        import numpy as np
        N_NODES = 6250
        N_EDGES = 100000

        def gat_layer(x, src, dst, W, a_s, a_d, b, concat):
            N = x.shape[0]
            H, C = a_s.shape
            h = (x @ W).reshape(N, H, C)
            alpha_s = jnp.einsum('nhc,hc->nh', h, a_s)
            alpha_d = jnp.einsum('nhc,hc->nh', h, a_d)
            logits = jax.nn.leaky_relu(alpha_s[src] + alpha_d[dst], 0.2)
            m = jax.ops.segment_max(logits, dst, num_segments=N)
            e = jnp.exp(logits - m[dst])
            s = jax.ops.segment_sum(e, dst, num_segments=N)
            a = e / s[dst]
            out = jax.ops.segment_sum(h[src] * a[:, :, None], dst, num_segments=N)
            out = out.reshape(N, H * C) if concat else out.mean(axis=1)
            return out + b
        key = jax.random.key(seed)
        ks = jax.random.split(key, 10)
        in_c, hid, heads, out_c = (64, 64, 2, 64)
        x = jax.random.normal(ks[0], (N_NODES, in_c), dtype=jnp.float32)
        edge_index = jax.random.randint(ks[1], (2, N_EDGES), 0, N_NODES, dtype=jnp.int64)
        sc = lambda f: 1.0 / np.sqrt(f)
        W1 = jax.random.normal(ks[2], (in_c, heads * hid), dtype=jnp.float32) * sc(in_c)
        as1 = jax.random.normal(ks[3], (heads, hid), dtype=jnp.float32) * sc(hid)
        ad1 = jax.random.normal(ks[4], (heads, hid), dtype=jnp.float32) * sc(hid)
        b1 = jnp.zeros((heads * hid,), dtype=jnp.float32)
        W2 = jax.random.normal(ks[5], (heads * hid, heads * out_c), dtype=jnp.float32) * sc(heads * hid)
        as2 = jax.random.normal(ks[6], (heads, out_c), dtype=jnp.float32) * sc(out_c)
        ad2 = jax.random.normal(ks[7], (heads, out_c), dtype=jnp.float32) * sc(out_c)
        b2 = jnp.zeros((out_c,), dtype=jnp.float32)
        return {'x': x, 'edge_index': edge_index, 'W1': W1, 'as1': as1, 'ad1': ad1, 'b1': b1, 'W2': W2, 'as2': as2, 'ad2': ad2, 'b2': b2}
    _L2_gnn_all = _L2_gnn_setup()
    _L2_gnn_in = {k: v for k, v in _L2_gnn_all.items() if k in ('W1', 'as1', 'ad1', 'b1', 'W2', 'as2', 'ad2', 'b2')}
    del _L2_gnn_all

    def _L3_gnn_setup():
        import jax, jax.numpy as jnp
        import numpy as np
        N_NODES = 12500
        N_EDGES = 200000
        D_IN, D_HID, D_OUT = (64, 128, 64)

        def _sage_conv(x, src, dst, W_l, b, W_r, num_nodes):
            msg_sum = jax.ops.segment_sum(x[src], dst, num_segments=num_nodes)
            deg = jax.ops.segment_sum(jnp.ones((src.shape[0],), dtype=x.dtype), dst, num_segments=num_nodes)
            mean = msg_sum / jnp.maximum(deg, 1.0)[:, None]
            return mean @ W_l + b + x @ W_r
        key = jax.random.key(seed)
        ks = jax.random.split(key, 6)
        x = jax.random.normal(ks[0], (N_NODES, D_IN), dtype=jnp.float32)
        edge_index = jax.random.randint(ks[1], (2, N_EDGES), 0, N_NODES, dtype=jnp.int64)
        s_in = 1.0 / np.sqrt(D_IN)
        s_hid = 1.0 / np.sqrt(D_HID)
        return {'x': x, 'edge_index': edge_index, 'W1_l': jax.random.normal(ks[2], (D_IN, D_HID), dtype=jnp.float32) * s_in, 'b1': jnp.zeros((D_HID,), dtype=jnp.float32), 'W1_r': jax.random.normal(ks[3], (D_IN, D_HID), dtype=jnp.float32) * s_in, 'W2_l': jax.random.normal(ks[4], (D_HID, D_OUT), dtype=jnp.float32) * s_hid, 'b2': jnp.zeros((D_OUT,), dtype=jnp.float32), 'W2_r': jax.random.normal(ks[5], (D_HID, D_OUT), dtype=jnp.float32) * s_hid}
    _L3_gnn_all = _L3_gnn_setup()
    _L3_gnn_in = {k: v for k, v in _L3_gnn_all.items() if k in ('W1_l', 'b1', 'W1_r', 'W2_l', 'b2', 'W2_r')}
    del _L3_gnn_all
    return {'x': x, 'src': src, 'dst': dst, 'edge_type_65': edge_type_65, 'L0_gnn_W': _L0_gnn_in['W'], 'L0_gnn_root': _L0_gnn_in['root'], 'L0_gnn_bias': _L0_gnn_in['bias'], 'L0_gnn_res_W': _L0_gnn_in['res_W'], 'L0_gnn_res_b': _L0_gnn_in['res_b'], 'L1_gnn_W1': _L1_gnn_in['W1'], 'L1_gnn_b1': _L1_gnn_in['b1'], 'L1_gnn_W2': _L1_gnn_in['W2'], 'L1_gnn_b2': _L1_gnn_in['b2'], 'L1_gnn_gamma': _L1_gnn_in['gamma'], 'L1_gnn_beta': _L1_gnn_in['beta'], 'L2_gnn_W1': _L2_gnn_in['W1'], 'L2_gnn_as1': _L2_gnn_in['as1'], 'L2_gnn_ad1': _L2_gnn_in['ad1'], 'L2_gnn_b1': _L2_gnn_in['b1'], 'L2_gnn_W2': _L2_gnn_in['W2'], 'L2_gnn_as2': _L2_gnn_in['as2'], 'L2_gnn_ad2': _L2_gnn_in['ad2'], 'L2_gnn_b2': _L2_gnn_in['b2'], 'L3_gnn_W1_l': _L3_gnn_in['W1_l'], 'L3_gnn_b1': _L3_gnn_in['b1'], 'L3_gnn_W1_r': _L3_gnn_in['W1_r'], 'L3_gnn_W2_l': _L3_gnn_in['W2_l'], 'L3_gnn_b2': _L3_gnn_in['b2'], 'L3_gnn_W2_r': _L3_gnn_in['W2_r']}

def reference(x, src, dst, edge_type_65, L0_gnn_W, L0_gnn_root, L0_gnn_bias, L0_gnn_res_W, L0_gnn_res_b, L1_gnn_W1, L1_gnn_b1, L1_gnn_W2, L1_gnn_b2, L1_gnn_gamma, L1_gnn_beta, L2_gnn_W1, L2_gnn_as1, L2_gnn_ad1, L2_gnn_b1, L2_gnn_W2, L2_gnn_as2, L2_gnn_ad2, L2_gnn_b2, L3_gnn_W1_l, L3_gnn_b1, L3_gnn_W1_r, L3_gnn_W2_l, L3_gnn_b2, L3_gnn_W2_r):
    import jax
    import jax.numpy as jnp

    def _L0_gnn_ref(x, edge_index, edge_type, W, root, bias, res_W, res_b):
        import jax, jax.numpy as jnp
        import numpy as np
        N, E, D, R, L = (6250, 75000, 64, 65, 2)

        def _rgcn_conv(x, src, dst, edge_type, W_r, W_root, b):
            n, d = x.shape
            r = W_r.shape[0]
            seg = dst * r + edge_type
            msg = x[src]
            agg = jax.ops.segment_sum(msg, seg, num_segments=n * r).reshape(n, r, d)
            cnt = jax.ops.segment_sum(jnp.ones((msg.shape[0],), x.dtype), seg, num_segments=n * r).reshape(n, r, 1)
            mean = agg / jnp.maximum(cnt, 1.0)
            out = jnp.einsum('nrd,rdk->nk', mean, W_r)
            return out + x @ W_root + b
        src, dst = (edge_index[0], edge_index[1])
        h = x
        for l in range(W.shape[0]):
            conv = _rgcn_conv(h, src, dst, edge_type, W[l], root[l], bias[l])
            conv = jax.nn.relu(conv)
            res = jax.nn.relu(h @ res_W[l] + res_b[l])
            h = conv + res
        return h

    def _L1_gnn_ref(x, edge_index, W1, b1, W2, b2, gamma, beta):
        import jax, jax.numpy as jnp
        import numpy as np
        N = 12500
        E = 200000
        IN_DIM = 64
        OUT_DIM = 64
        BN_EPS = 1e-05
        row, col = (edge_index[0], edge_index[1])
        keep = (row != col).astype(x.dtype)[:, None]
        x_j = x[col] * keep
        agg = jax.ops.segment_sum(x_j, row, num_segments=x.shape[0])
        h = x + agg
        h = jax.nn.relu(h @ W1 + b1)
        h = jax.nn.relu(h @ W2 + b2)
        mean = jnp.mean(h, axis=0)
        var = jnp.mean(jnp.square(h - mean), axis=0)
        out = (h - mean) * jax.lax.rsqrt(var + BN_EPS) * gamma + beta
        return out

    def _L2_gnn_ref(x, edge_index, W1, as1, ad1, b1, W2, as2, ad2, b2):
        import jax, jax.numpy as jnp
        import numpy as np
        N_NODES = 6250
        N_EDGES = 100000

        def gat_layer(x, src, dst, W, a_s, a_d, b, concat):
            N = x.shape[0]
            H, C = a_s.shape
            h = (x @ W).reshape(N, H, C)
            alpha_s = jnp.einsum('nhc,hc->nh', h, a_s)
            alpha_d = jnp.einsum('nhc,hc->nh', h, a_d)
            logits = jax.nn.leaky_relu(alpha_s[src] + alpha_d[dst], 0.2)
            m = jax.ops.segment_max(logits, dst, num_segments=N)
            e = jnp.exp(logits - m[dst])
            s = jax.ops.segment_sum(e, dst, num_segments=N)
            a = e / s[dst]
            out = jax.ops.segment_sum(h[src] * a[:, :, None], dst, num_segments=N)
            out = out.reshape(N, H * C) if concat else out.mean(axis=1)
            return out + b
        N = x.shape[0]
        loops = jnp.arange(N, dtype=edge_index.dtype)
        src = jnp.concatenate([edge_index[0], loops])
        dst = jnp.concatenate([edge_index[1], loops])
        h = gat_layer(x, src, dst, W1, as1, ad1, b1, concat=True)
        out = gat_layer(h, src, dst, W2, as2, ad2, b2, concat=False)
        return out

    def _L3_gnn_ref(x, edge_index, W1_l, b1, W1_r, W2_l, b2, W2_r):
        import jax, jax.numpy as jnp
        import numpy as np
        N_NODES = 12500
        N_EDGES = 200000
        D_IN, D_HID, D_OUT = (64, 128, 64)

        def _sage_conv(x, src, dst, W_l, b, W_r, num_nodes):
            msg_sum = jax.ops.segment_sum(x[src], dst, num_segments=num_nodes)
            deg = jax.ops.segment_sum(jnp.ones((src.shape[0],), dtype=x.dtype), dst, num_segments=num_nodes)
            mean = msg_sum / jnp.maximum(deg, 1.0)[:, None]
            return mean @ W_l + b + x @ W_r
        src, dst = (edge_index[0], edge_index[1])
        n = x.shape[0]
        h = jax.nn.relu(_sage_conv(x, src, dst, W1_l, b1, W1_r, n))
        out = _sage_conv(h, src, dst, W2_l, b2, W2_r, n)
        return out
    edge_index = jnp.stack([src, dst])
    x = _layernorm(x + _L0_gnn_ref(x, edge_index, edge_type_65, L0_gnn_W, L0_gnn_root, L0_gnn_bias, L0_gnn_res_W, L0_gnn_res_b), axis=-1)
    x = _layernorm(x + _L1_gnn_ref(x, edge_index, L1_gnn_W1, L1_gnn_b1, L1_gnn_W2, L1_gnn_b2, L1_gnn_gamma, L1_gnn_beta), axis=-1)
    x = _layernorm(x + _L2_gnn_ref(x, edge_index, L2_gnn_W1, L2_gnn_as1, L2_gnn_ad1, L2_gnn_b1, L2_gnn_W2, L2_gnn_as2, L2_gnn_ad2, L2_gnn_b2), axis=-1)
    x = _layernorm(x + _L3_gnn_ref(x, edge_index, L3_gnn_W1_l, L3_gnn_b1, L3_gnn_W1_r, L3_gnn_W2_l, L3_gnn_b2, L3_gnn_W2_r), axis=-1)
    return x

_drawn_inputs = setup_inputs


def setup_inputs(seed=0):
    import zlib

    import numpy as np

    out = dict(_drawn_inputs(seed))
    spreads = {'L1_gnn_b1': (0.0, 0.351),
     'L1_gnn_b2': (0.0, 0.1),
     'L1_gnn_gamma': (1.0, 0.2),
     'L1_gnn_beta': (0.0, 0.1),
     'L2_gnn_b1': (0.0, 0.1),
     'L2_gnn_b2': (0.0, 0.1),
     'L3_gnn_b1': (0.0, 0.1),
     'L3_gnn_b2': (0.0, 0.1)}
    factors = {'L0_gnn_bias': 8.0,
     'L0_gnn_res_b': 8.0,
     'L2_gnn_ad1': 4.14,
     'L2_gnn_as2': 5.316,
     'L2_gnn_ad2': 8.0}
    for name, (base, spread) in spreads.items():
        noise = np.random.default_rng([zlib.crc32(name.encode()), seed]).standard_normal(out[name].shape)
        drawn = base * np.exp(spread * noise) if base else spread * noise
        out[name] = jnp.asarray(drawn.astype(out[name].dtype))
    for name, factor in factors.items():
        out[name] = (out[name] * factor).astype(out[name].dtype)
    return out
```

```python
import concourse.bass as bass
from concourse import mybir
from contextlib import ExitStack, contextmanager

P = 128
N = 6250
E = 206250
D = 64
R = 65
NB = -(-N // P)
LAST = N - (NB - 1) * P
PADNODE = NB * P
KEYS = NB + 1
EC = -(-E // P)
ETAIL = E - (P - 1) * EC
GRP = 8
PAIRS = -(-(EC + KEYS) // (2 * GRP))
CH = PAIRS * 2 * GRP
NTAB = KEYS * P
GW = 132
HW = D + 1
NEG = -3.0e38
SC = 13
assert EC % (2 * SC) == 0

fp32, bf16, i32 = mybir.dt.float32, mybir.dt.bfloat16, mybir.dt.int32
ALU = mybir.AluOpType
ACT = mybir.ActivationFunctionType
AX = mybir.AxisListType


def later(i):
    return not (isinstance(i, int) and i == 0)


def rounds(eng, n, body):
    body(0)
    with eng.Fori(1, n) as i:
        body(i)


class Order:

    def __init__(self, eng, sem, base=0):
        self.eng, self.sem, self.base, self.n = eng, sem, base, 0

    def link(self, ins):
        self.n += 1
        ins.then_inc(self.sem, 1)
        self.eng.wait_ge(self.sem, self.base + self.n)


class Chip:

    def __init__(self, nc, ctx):
        self.nc, self.ctx = nc, ctx
        self.stages = 0
        self.bank = [ctx.enter_context(nc.psum_tensor(f"bank{i}", [P, 512], fp32)) for i in range(8)]

    def keep(self, name, shape, dt):
        return self.ctx.enter_context(self.nc.sbuf_tensor(name, shape, dt))

    @contextmanager
    def stage(self, name, *sems):
        self.stages += 1
        handles = [self.nc.alloc_semaphore(f"{name}{self.stages}_{s}") for s in sems]
        with self.nc.Block() as block:
            yield (block, *handles)
        self.nc.clear_and_free_semaphores(handles)
        self.nc.all_engine_barrier(sem_only=True)


def constants(c):
    nc = c.nc
    c.iota = c.keep("iota", [P, P], fp32)
    c.keyno = c.keep("keyno", [P, KEYS], fp32)
    c.ident = c.keep("ident", [P, P], fp32)
    c.identb = c.keep("identb", [P, P], bf16)
    c.ones = c.keep("ones", [P, P], fp32)
    c.lower = c.keep("lower", [P, P], fp32)
    c.chunkno = c.keep("chunkno", [P, CH // P], fp32)
    c.rowno = c.keep("rowno", [P, 1], fp32)
    c.valid = c.keep("valid", [P, 1], fp32)
    with c.stage("const", "made", "step") as (block, made, step):
        @block.gpsimd
        def _(pool):
            nc.gpsimd.iota(c.iota[:, :], pattern=[[1, P]], base=0, channel_multiplier=0,
                           allow_small_or_imprecise_dtypes=True).then_inc(made, 1)
            nc.gpsimd.iota(c.keyno[:, :], pattern=[[1, KEYS]], base=0, channel_multiplier=0,
                           allow_small_or_imprecise_dtypes=True).then_inc(made, 1)
            nc.gpsimd.iota(c.chunkno[:, :], pattern=[[1, CH // P]], base=0, channel_multiplier=CH // P,
                           allow_small_or_imprecise_dtypes=True).then_inc(made, 1)
            nc.gpsimd.iota(c.rowno[:, :], pattern=[[1, 1]], base=0, channel_multiplier=1,
                           allow_small_or_imprecise_dtypes=True).then_inc(made, 1)
            nc.gpsimd.memset(c.ones[:, :], 1.0).then_inc(made, 1)

        @block.vector
        def _(dve):
            dve.wait_ge(made, 5)
            nc.vector.tensor_scalar(c.ident[:, :], c.iota[:, :], c.rowno[:, 0:1], None, ALU.is_equal).then_inc(step, 1)
            nc.vector.tensor_scalar(c.lower[:, :], c.iota[:, :], c.rowno[:, 0:1], None, ALU.is_gt).then_inc(step, 1)
            nc.vector.tensor_scalar(c.valid[:, :], c.rowno[:, :], float(LAST), None, ALU.is_lt).then_inc(step, 1)
            dve.wait_ge(step, 1)
            nc.vector.tensor_copy(c.identb[:, :], c.ident[:, :]).then_inc(step, 1)


class Edges:

    def __init__(self, c, name, typed):
        self.node = c.keep(f"{name}_node", [P, CH], i32)
        self.local = c.keep(f"{name}_local", [P, CH], fp32)
        self.block = c.keep(f"{name}_block", [1, CH], i32)
        if typed:
            self.row = c.keep(f"{name}_row", [P, CH], i32)
            self.relation = c.keep(f"{name}_relation", [P, CH], fp32)
            self.weight = c.keep(f"{name}_weight", [P, CH], fp32)


def sort_edges(c, name, key, other, relation, listed, blocks_dram, out):
    nc = c.nc
    ctx = ExitStack()

    def tmp(n, shape, dt):
        return ctx.enter_context(nc.sbuf_tensor(f"{name}_{n}", shape, dt))

    with ctx:
        keyv = tmp("key", [P, EC], i32)
        othv = tmp("other", [P, EC], i32)
        relv = tmp("relation", [P, EC], i32) if relation is not None else None
        keyb = tmp("keyblock", [P, EC], i32)
        keyf = tmp("keyblockf", [P, EC], fp32)
        eq = tmp("is_key", [P, EC], i32)
        cum = tmp("running", [P, EC], fp32)
        pos = tmp("slot", [P, EC], fp32)
        dest = tmp("dest", [P, EC], i32)
        rec = tmp("records", [P, CH, 4], i32)
        total = tmp("total", [P, KEYS], fp32)
        chunks = tmp("chunks", [P, KEYS], fp32)
        chunki = tmp("chunki", [P, KEYS], i32)
        upto = tmp("upto", [P, KEYS], fp32)
        first = tmp("first", [P, KEYS], fp32)
        start = tmp("start", [P, KEYS], fp32)
        zero = tmp("zero", [P, KEYS], fp32)
        owner = tmp("owner", [P, CH // P], fp32)
        owneri = tmp("owneri", [P, CH // P], i32)
        blank = tmp("blank", [P, CH // 16, 4], i32)
        ib = tmp("scatter_index", [P, 2, SC], i32)
        rb = tmp("scatter_rows", [P, 2, SC, 4], i32)
        before, overall = c.bank[0][:, 0:KEYS], c.bank[1][:, 0:KEYS]
        loads = 3 if relation is not None else 2

        with c.stage(name, "filled", "loaded", "blanked", "step", "totalled", "placed", "summed", "started",
                     "owned", "ownerout", "ownerin", "copied", "sent0", "sent1", "back", "placing") as (
                block, filled, loaded, blanked, step, totalled, placed, summed, started,
                owned, ownerout, ownerin, copied, sent0, sent1, back, placing):
            sent = [sent0, sent1]

            @block.sync
            def _(sp):
                sp.wait_ge(filled, 2 * loads + 2)
                for dst_sb, src_dram in ((keyv, key), (othv, other), (relv, relation)):
                    if dst_sb is not None:
                        sp.dma_start(dst_sb[0:P - 1, :],
                                     src_dram[0:(P - 1) * EC].rearrange("(p c) -> p c", c=EC)).then_inc(loaded, 16)
                        sp.dma_start(dst_sb[P - 1:P, 0:ETAIL],
                                     src_dram[(P - 1) * EC:E].rearrange("(p c) -> p c", p=1)).then_inc(loaded, 16)
                for k in range(16):
                    sp.dma_start(listed[:, k * (CH // 16) * 4:(k + 1) * (CH // 16) * 4],
                                 blank[:, :, :].rearrange("p c w -> p (c w)")).then_inc(blanked, 16)
                sp.wait_ge(owned, 1)
                sp.dma_start(blocks_dram.rearrange("(p c) -> p c", p=P), owneri[:, :]).then_inc(ownerout, 16)
                sp.wait_ge(ownerout, 16)
                sp.dma_start(out.block[0:1, :], blocks_dram.rearrange("(a c) -> a c", a=1)).then_inc(ownerin, 16)
                sp.wait_ge(ownerin, 16)
                sp.wait_ge(sent0, 16 * SC * (EC // (2 * SC)))
                sp.wait_ge(sent1, 16 * SC * (EC // (2 * SC)))
                sp.dma_start(rec[:, :, :].rearrange("p c w -> p (c w)"), listed[0:P, :]).then_inc(back, 16)
                sp.wait_ge(back, 16)

            @block.gpsimd
            def _(pool):
                nc.gpsimd.memset(keyv[:, :], PADNODE).then_inc(filled, 1)
                nc.gpsimd.memset(othv[:, :], 0).then_inc(filled, 1)
                if relv is not None:
                    nc.gpsimd.memset(relv[:, :], 0).then_inc(filled, 1)
                nc.gpsimd.memset(blank[:, :, :], 0).then_inc(filled, 1)
                pool.wait_ge(filled, loads + 1)
                nc.gpsimd.memset(blank[:, :, 1:2], -1).then_inc(filled, loads + 1)
                pool.wait_ge(placed, 1)
                pool.wait_ge(blanked, 16 * 16)
                rows = listed.rearrange("p (c w) -> (p c) w", w=4)

                def scatter(i):
                    for h in range(2):
                        col = i * (2 * SC) + h * SC
                        if later(i):
                            pool.wait_ge(sent[h], i * (16 * SC))
                        nc.gpsimd.tensor_copy(ib[:, h, :], dest[:, bass.ds(col, SC)]).then_inc(copied, 1)
                        nc.gpsimd.tensor_copy(rb[:, h, :, :], rec[:, bass.ds(col, SC), :]).then_inc(copied, 1)
                        pool.wait_ge(copied, i * 4 + (2 * h + 2))
                        pool.sem_inc(started, 1)
                        for k in range(SC):
                            nc.gpsimd.indirect_dma_start(
                                rows, bass.IndirectOffsetOnAxis(ap=ib[:, h, k:k + 1], axis=0),
                                rb[:, h, k, :], None).then_inc(sent[h], 16)

                rounds(pool, EC // (2 * SC), scatter)

            @block.vector
            def _(dve):
                o = Order(dve, step)
                o.link(nc.vector.memset(zero[:, :], 0.0))
                o.link(nc.vector.memset(pos[:, :], 0.0))
                dve.wait_ge(loaded, 32 * loads)
                o.link(nc.vector.tensor_scalar(keyb[:, :], keyv[:, :], 7, None, ALU.logical_shift_right))
                o.link(nc.vector.tensor_copy(keyf[:, :], keyb[:, :]))

                def count(k):
                    ck = Order(dve, totalled, k)
                    ck.link(nc.vector.tensor_scalar(cum[:, :], keyf[:, :], c.keyno[:, bass.ds(k, 1)], 0.0,
                                                    ALU.is_equal, ALU.add, accum_out=total[:, bass.ds(k, 1)]))

                rounds(dve, KEYS, count)
                dve.wait_ge(summed, 1)
                o.link(nc.vector.tensor_scalar(chunki[:, :], overall, float(P - 1), None, ALU.add))
                o.link(nc.vector.tensor_scalar(chunki[:, :], chunki[:, :], 7, None, ALU.logical_shift_right))
                o.link(nc.vector.tensor_copy(chunks[:, :], chunki[:, :]))
                o.link(nc.vector.tensor_tensor_scan(upto[:, :], chunks[:, :], zero[:, :], 0.0, ALU.add, ALU.add))
                o.link(nc.vector.tensor_tensor(first[:, :], upto[:, :], chunks[:, :], ALU.subtract))
                o.link(nc.vector.tensor_scalar(start[:, :], first[:, :], float(P), -1.0, ALU.mult, ALU.add))
                o.link(nc.vector.tensor_tensor(start[:, :], start[:, :], before, ALU.add))
                o.link(nc.vector.memset(owner[:, :], 0.0))
                for k in range(1, KEYS):
                    o.link(nc.vector.scalar_tensor_tensor(owner[:, :], c.chunkno[:, :], first[:, k:k + 1],
                                                          owner[:, :], ALU.is_ge, ALU.add))
                nc.vector.tensor_copy(owneri[:, :], owner[:, :]).then_inc(owned, 1)

                def place(k):
                    pk = Order(dve, placing, k * 4)
                    pk.link(nc.vector.tensor_scalar(eq[:, :], keyf[:, :], c.keyno[:, bass.ds(k, 1)], None, ALU.is_equal))
                    pk.link(nc.vector.tensor_tensor_scan(cum[:, :], eq[:, :], eq[:, :], start[:, bass.ds(k, 1)],
                                                         ALU.add, ALU.bypass))
                    pk.link(nc.vector.tensor_tensor(cum[:, :], cum[:, :], eq[:, :], ALU.mult))
                    pk.link(nc.vector.tensor_tensor(pos[:, :], pos[:, :], cum[:, :], ALU.add))

                rounds(dve, KEYS, place)
                o.link(nc.vector.tensor_copy(dest[:, :], pos[:, :]))
                o.link(nc.vector.tensor_scalar(keyb[:, :], dest[:, :], 7, None, ALU.logical_shift_right))
                o.link(nc.vector.tensor_scalar(dest[:, :], dest[:, :], P - 1, None, ALU.bitwise_and))
                o.link(nc.vector.scalar_tensor_tensor(dest[:, :], dest[:, :], float(CH), keyb[:, :], ALU.mult, ALU.add))
                r = rec[:, 0:EC, :]
                o.link(nc.vector.tensor_copy(r[:, :, 0], othv[:, :]))
                o.link(nc.vector.tensor_scalar(r[:, :, 1], keyv[:, :], P - 1, None, ALU.bitwise_and))
                if relv is not None:
                    o.link(nc.vector.scalar_tensor_tensor(r[:, :, 2], othv[:, :], float(R), relv[:, :], ALU.mult, ALU.add))
                    nc.vector.tensor_copy(r[:, :, 3], relv[:, :]).then_inc(placed, 1)
                else:
                    o.link(nc.vector.tensor_tensor(eq[:, :], keyv[:, :], othv[:, :], ALU.not_equal))
                    o.link(nc.vector.scalar_tensor_tensor(keyb[:, :], r[:, :, 1], 1.0, eq[:, :], ALU.add, ALU.mult))
                    o.link(nc.vector.tensor_scalar(r[:, :, 1], keyb[:, :], -1.0, None, ALU.add))
                    o.link(nc.vector.memset(r[:, :, 2], 0))
                    nc.vector.memset(r[:, :, 3], 0).then_inc(placed, 1)
                dve.wait_ge(back, 16)
                nc.vector.tensor_copy(out.node[:, :], rec[:, :, 0]).then_inc(step, 1)
                nc.vector.tensor_copy(out.local[:, :], rec[:, :, 1]).then_inc(step, 1)
                if relv is not None:
                    nc.vector.tensor_copy(out.row[:, :], rec[:, :, 2]).then_inc(step, 1)
                    nc.vector.tensor_copy(out.relation[:, :], rec[:, :, 3]).then_inc(step, 1)

            @block.tensor
            def _(pe):
                pe.wait_ge(totalled, KEYS)
                nc.tensor.matmul(before, c.lower[:, :], total[:, :], start=True, stop=True)
                nc.tensor.matmul(overall, c.ones[:, :], total[:, :], start=True, stop=True).then_inc(summed, 1)


def chunk_blocks(eng, row, g):
    return [eng.value_load(row[0:1, bass.ds(g * GRP + k, 1)], min_val=0, max_val=KEYS - 1) for k in range(GRP)]


def pipeline(eng, step, drain=None):
    def both(i):
        step(i, 0, i, 1)
        step(i, 1, i + 1, 0)

    rounds(eng, PAIRS - 1, both)
    step(PAIRS - 1, 0, PAIRS - 1, 1)
    step(PAIRS - 1, 1, None, None)
    if drain:
        drain(PAIRS - 1, 1)


def before(i, h):
    return (i, 0) if h else (i - 1, 1)


def gather_groups(nc, pool, table, idx, ib, G, gathered, free, copied, started):
    def one(i):
        for h in range(2):
            if later(i):
                pool.wait_ge(free[h], i)
            nc.gpsimd.tensor_copy(ib[:, h, :], idx[:, bass.ds(i * (2 * GRP) + h * GRP, GRP)]).then_inc(copied, 1)
            pool.wait_ge(copied, i * 2 + (h + 1))
            pool.sem_inc(started, 1)
            for k in range(GRP):
                nc.gpsimd.indirect_dma_start(G[:, h, k, :], None, table,
                                             bass.IndirectOffsetOnAxis(ap=ib[:, h, k:k + 1], axis=0)
                                             ).then_inc(gathered[h], 16)

    rounds(pool, PAIRS, one)
    for h in range(2):
        pool.wait_ge(gathered[h], 16 * GRP * PAIRS)


def edge_pass(c, name, table, idx, edges, acc, weighted=False):
    nc = c.nc
    width = table.shape[-1]
    with (nc.sbuf_tensor(f"{name}_G", [P, 2, GRP, width], fp32) as G,
          nc.sbuf_tensor(f"{name}_onehot", [P, 2, GRP, P], fp32) as onehot,
          nc.sbuf_tensor(f"{name}_ib", [P, 2, GRP], i32) as ib,
          c.stage(name, "gathered0", "gathered1", "used0", "used1", "copied", "started", "marked0", "marked1",
                  "added") as (block, gathered0, gathered1, used0, used1, copied, started, marked0, marked1, added)):
        gathered, used, marked = (gathered0, gathered1), (used0, used1), (marked0, marked1)

        @block.gpsimd
        def _(pool):
            gather_groups(nc, pool, table, idx, ib, G, gathered, used, copied, started)

        @block.vector
        def _(dve):
            def mark(i, h):
                if later(i):
                    dve.wait_ge(used[h], i)
                for k in range(GRP):
                    at = bass.ds(i * (2 * GRP) + (h * GRP + k), 1)
                    if weighted:
                        last = nc.vector.tensor_scalar(onehot[:, h, k, :], c.iota[:, :], edges.local[:, at],
                                                       edges.weight[:, at], ALU.is_equal, ALU.mult)
                    else:
                        last = nc.vector.tensor_scalar(onehot[:, h, k, :], c.iota[:, :], edges.local[:, at],
                                                       None, ALU.is_equal)
                last.then_inc(marked[h], 1)

            def add(i, h):
                b = chunk_blocks(dve, edges.block, i * 2 + h)
                dve.wait_ge(used[h], i + 1)
                o = Order(dve, added, i * (2 * GRP) + h * GRP)
                for k in range(GRP):
                    o.link(nc.vector.tensor_tensor(acc[:, bass.ds(b[k], 1), :], acc[:, bass.ds(b[k], 1), :],
                                                   c.bank[h][:, k * width:(k + 1) * width].rearrange(
                                                       "p (a w) -> p a w", a=1), ALU.add))

            def step(i, h, ni, nh):
                if ni is not None:
                    mark(ni, nh)
                add(i, h)

            mark(0, 0)
            pipeline(dve, step)

        @block.tensor
        def _(pe):
            def products(i):
                for h in range(2):
                    pe.wait_ge(marked[h], i + 1)
                    pe.wait_ge(gathered[h], i * (16 * GRP) + 16 * GRP)
                    if later(i):
                        pe.wait_ge(added, i * (2 * GRP) - GRP + h * GRP)
                    for k in range(GRP):
                        last = nc.tensor.matmul(c.bank[h][:, k * width:(k + 1) * width], onehot[:, h, k, :],
                                                G[:, h, k, :], start=True, stop=True)
                    last.then_inc(used[h], 1)

            rounds(pe, PAIRS, products)


def relation_weights(c, edges, counts):
    nc = c.nc
    HB = GRP // 2
    with (nc.sbuf_tensor("cw_onehot", [P, 2, GRP, P], bf16) as onehot,
          nc.sbuf_tensor("cw_turned", [P, 2, GRP, P], fp32) as onehotT,
          nc.sbuf_tensor("cw_relation", [P, 2, GRP, R], bf16) as rel,
          nc.sbuf_tensor("cw_picked", [P, 2, GRP, R], fp32) as picked):

        def mark_both(dve, i, h, marked):
            for k in range(GRP):
                at = bass.ds(i * (2 * GRP) + (h * GRP + k), 1)
                nc.vector.tensor_scalar(onehot[:, h, k, :], c.iota[:, :], edges.local[:, at], None, ALU.is_equal)
                last = nc.vector.tensor_scalar(rel[:, h, k, :], c.iota[:, 0:R], edges.relation[:, at], None,
                                               ALU.is_equal)
            last.then_inc(marked[h], 1)

        with c.stage("count", "used0", "used1", "marked0", "marked1", "added", "cleared") as (
                block, used0, used1, marked0, marked1, added, cleared):
            used, marked = (used0, used1), (marked0, marked1)

            @block.vector
            def _(dve):
                nc.vector.memset(counts[:, :, :], 0.0).then_inc(cleared, 1)
                dve.wait_ge(cleared, 1)

                def mark(i, h):
                    if later(i):
                        dve.wait_ge(used[h], i)
                    mark_both(dve, i, h, marked)

                def add(i, h):
                    b = chunk_blocks(dve, edges.block, i * 2 + h)
                    dve.wait_ge(used[h], i + 1)
                    o = Order(dve, added, i * (2 * GRP) + h * GRP)
                    for k in range(GRP):
                        at = (k % HB) * R
                        o.link(nc.vector.tensor_tensor(
                            counts[:, bass.ds(b[k], 1), :], counts[:, bass.ds(b[k], 1), :],
                            c.bank[2 * h + k // HB][:, at:at + R].rearrange("p (a w) -> p a w", a=1), ALU.add))

                def step(i, h, ni, nh):
                    if ni is not None:
                        mark(ni, nh)
                    add(i, h)

                mark(0, 0)
                pipeline(dve, step)

            @block.tensor
            def _(pe):
                def products(i):
                    for h in range(2):
                        pe.wait_ge(marked[h], i + 1)
                        if later(i):
                            pe.wait_ge(added, i * (2 * GRP) - GRP + h * GRP)
                        for k in range(GRP):
                            at = (k % HB) * R
                            last = nc.tensor.matmul(c.bank[2 * h + k // HB][:, at:at + R], onehot[:, h, k, :],
                                                    rel[:, h, k, :], start=True, stop=True)
                        last.then_inc(used[h], 1)

                rounds(pe, PAIRS, products)

        with c.stage("weigh", "marked0", "marked1", "turned0", "turned1", "spread0", "spread1", "looked0",
                     "looked1", "picked") as (block, marked0, marked1, turned0, turned1, spread0, spread1,
                                              looked0, looked1, pick):
            marked, turned, spread, looked = (marked0, marked1), (turned0, turned1), (spread0, spread1), (looked0, looked1)

            @block.vector
            def _(dve):
                def mark(i, h):
                    if later(i):
                        dve.wait_ge(turned[h], i)
                    mark_both(dve, i, h, marked)

                def choose(i, h):
                    dve.wait_ge(looked[h], i + 1)
                    o = Order(dve, pick, i * 6 + h * 3)
                    for q in range(2):
                        o.link(nc.vector.tensor_tensor(
                            picked[:, h, q * HB:(q + 1) * HB, :],
                            c.bank[2 * h + q][:, 0:HB * R].rearrange("p (k r) -> p k r", r=R),
                            rel[:, h, q * HB:(q + 1) * HB, :], ALU.mult))
                    o.link(nc.vector.tensor_reduce(edges.weight[:, bass.ds(i * (2 * GRP) + h * GRP, GRP)],
                                                   picked[:, h, :, :], AX.X, ALU.add))

                def step(i, h, ni, nh):
                    if ni is not None:
                        mark(ni, nh)
                    choose(i, h)

                mark(0, 0)
                pipeline(dve, step)
                o = Order(dve, pick, 6 * PAIRS)
                o.link(nc.vector.tensor_scalar(edges.weight[:, :], edges.weight[:, :], 1.0, None, ALU.max))
                nc.vector.reciprocal(edges.weight[:, :], edges.weight[:, :]).then_inc(pick, 1)

            @block.scalar
            def _(act):
                def spread_out(i):
                    for h in range(2):
                        act.wait_ge(turned[h], i + 1)
                        if later(i):
                            act.wait_ge(looked[h], i)
                        nc.scalar.activation(onehotT[:, h, :, :].rearrange("p k n -> p (k n)"),
                                             c.bank[6 + h][:, :].bitcast(bf16), ACT.Copy).then_inc(spread[h], 1)

                rounds(act, PAIRS, spread_out)

            @block.tensor
            def _(pe):
                def turn(i, h):
                    pe.wait_ge(marked[h], i + 1)
                    if later(i):
                        pe.wait_ge(spread[h], i)
                    for k in range(GRP):
                        last = nc.tensor.transpose(c.bank[6 + h][:, :].bitcast(bf16)[:, k * P:(k + 1) * P],
                                                   onehot[:, h, k, :], c.identb[:, :])
                    last.then_inc(turned[h], 1)

                def look(i, h):
                    b = chunk_blocks(pe, edges.block, i * 2 + h)
                    pe.wait_ge(spread[h], i + 1)
                    if later(i):
                        pe.wait_ge(pick, i * 6 - 3 + h * 3)
                    for k in range(GRP):
                        at = (k % HB) * R
                        last = nc.tensor.matmul(c.bank[2 * h + k // HB][:, at:at + R], onehotT[:, h, k, :],
                                                counts[:, bass.ds(b[k], 1), :].rearrange("p a r -> p (a r)"),
                                                start=True, stop=True)
                    last.then_inc(looked[h], 1)

                def step(i, h, ni, nh):
                    if ni is not None:
                        turn(ni, nh)
                    look(i, h)

                turn(0, 0)
                pipeline(pe, step)


def block_rounds(eng, one):
    def both(i):
        one(i, 0)
        one(i, 1)

    rounds(eng, NB // 2, both)
    if NB % 2:
        one(NB // 2, 0)


def node_product(c, name, src, weight, out):
    nc = c.nc
    K, M = src.shape[-1], weight.shape[-1]
    with (nc.sbuf_tensor(f"{name}_x", [P, 2, P], fp32) as xb,
          nc.sbuf_tensor(f"{name}_xT", [K, 2, P], fp32) as xT,
          c.stage(name, "blanked", "taken0", "taken1", "turned0", "turned1", "lifted0", "lifted1", "made0", "made1",
                  "out0", "out1") as (block, blanked, taken0, taken1, turned0, turned1, lifted0, lifted1,
                                      made0, made1, out0, out1)):
        taken, turned, lifted = (taken0, taken1), (turned0, turned1), (lifted0, lifted1)
        made, stored = (made0, made1), (out0, out1)

        @block.gpsimd
        def _(pool):
            nc.gpsimd.memset(xb[:, :, :], 0.0).then_inc(blanked, 1)

        @block.scalar
        def _(act):
            def take(i, h):
                if later(i):
                    act.wait_ge(turned[h], i)
                nc.scalar.activation(xb[:, h, 0:K], src[:, bass.ds(i * 2 + h, 1), :].rearrange("p a k -> p (a k)"),
                                     ACT.Copy).then_inc(taken[h], 1)

            act.wait_ge(blanked, 1)
            block_rounds(act, take)

        @block.vector
        def _(dve):
            def lift(i, h):
                dve.wait_ge(turned[h], i + 1)
                if later(i):
                    dve.wait_ge(made[h], i)
                nc.vector.tensor_copy(xT[:, h, :], c.bank[h][0:K, 0:P]).then_inc(lifted[h], 1)

            def store(i, h):
                dve.wait_ge(made[h], i + 1)
                nc.vector.tensor_copy(out[:, bass.ds(i * 2 + h, 1), :],
                                      c.bank[2 + h][:, 0:M].rearrange("p (a m) -> p a m", a=1)).then_inc(stored[h], 1)

            def one(i, h):
                lift(i, h)
                if later(i) or h:
                    store(*before(i, h))

            block_rounds(dve, one)
            store(NB // 2, 0)

        @block.tensor
        def _(pe):
            def turn(i, h):
                pe.wait_ge(taken[h], i + 1)
                if later(i):
                    pe.wait_ge(lifted[h], i)
                nc.tensor.transpose(c.bank[h][:, 0:P], xb[:, h, :], c.ident[:, :]).then_inc(turned[h], 1)

            def product(i, h):
                pe.wait_ge(lifted[h], i + 1)
                if later(i):
                    pe.wait_ge(stored[h], i)
                nc.tensor.matmul(c.bank[2 + h][:, 0:M], xT[:, h, :], weight, start=True, stop=True).then_inc(made[h], 1)

            def one(i, h):
                turn(i, h)
                if later(i) or h:
                    product(*before(i, h))

            block_rounds(pe, one)
            product(NB // 2, 0)


PIECES = 10
PW = R * D // PIECES
assert PW * PIECES == R * D and PW <= 512
RING = PIECES // 2


def relation_table(c, name, src, weight, table):
    nc = c.nc
    with (nc.sbuf_tensor(f"{name}_x", [P, 2, P], fp32) as xb,
          nc.sbuf_tensor(f"{name}_xT", [D, 2, P], fp32) as xT,
          nc.sbuf_tensor(f"{name}_w", [D, R, D], fp32) as w,
          nc.sbuf_tensor(f"{name}_y", [P, 2, R * D], fp32) as y,
          c.stage(name, "weights", "blanked", "taken0", "taken1", "turned0", "turned1", "lifted0", "lifted1", "made",
                  "even", "odd", "sent0", "sent1") as (
                      block, weights, blanked, taken0, taken1, turned0, turned1, lifted0, lifted1, made,
                      even, odd, sent0, sent1)):
        taken, turned, lifted, sent = (taken0, taken1), (turned0, turned1), (lifted0, lifted1), (sent0, sent1)
        HP = PIECES // 2
        wf = w[:, :, :].rearrange("d r k -> d (r k)")

        @block.gpsimd
        def _(pool):
            nc.gpsimd.memset(xb[:, :, :], 0.0).then_inc(blanked, 1)

        @block.sync
        def _(sp):
            sp.dma_start(w[:, :, :], weight.rearrange("r d k -> d r k")).then_inc(weights, 16)

            def send(i, h):
                sp.wait_ge(even, i * (2 * HP) + (h + 1) * HP)
                sp.wait_ge(odd, i * (2 * HP) + (h + 1) * HP)
                sp.dma_start(table[bass.ds(i * 2 * P + h * P, P), :], y[:, h, :]).then_inc(sent[h], 16)

            block_rounds(sp, send)
            sp.wait_ge(sent[0], 16 * (NB // 2 + 1))
            sp.wait_ge(sent[1], 16 * (NB // 2))

        def store_piece(eng, copy, i, h, j):
            eng.wait_ge(made, i * (2 * PIECES) + (h * PIECES + j + 1))
            if later(i) and j < 2:
                eng.wait_ge(sent[h], i * 16)
            return copy(y[:, h, j * PW:(j + 1) * PW], c.bank[2 + j % RING][:, 0:PW])

        @block.scalar
        def _(act):
            def one(i, h):
                if later(i):
                    act.wait_ge(turned[h], i)
                nc.scalar.activation(xb[:, h, 0:D], src[:, bass.ds(i * 2 + h, 1), :].rearrange("p a k -> p (a k)"),
                                     ACT.Copy).then_inc(taken[h], 1)

            def pieces(i, h):
                for j in range(1, PIECES, 2):
                    store_piece(act, lambda o, s: nc.scalar.activation(o, s, ACT.Copy), i, h, j).then_inc(odd, 1)

            def step(i, h):
                one(i, h)
                if later(i) or h:
                    pieces(*before(i, h))

            act.wait_ge(blanked, 1)
            block_rounds(act, step)
            pieces(NB // 2, 0)

        @block.vector
        def _(dve):
            def lift(i, h):
                dve.wait_ge(turned[h], i + 1)
                if later(i):
                    dve.wait_ge(made, i * (2 * PIECES) - PIECES + h * PIECES)
                nc.vector.tensor_copy(xT[:, h, :], c.bank[h][0:D, 0:P]).then_inc(lifted[h], 1)

            def pieces(i, h):
                for j in range(0, PIECES, 2):
                    store_piece(dve, nc.vector.tensor_copy, i, h, j).then_inc(even, 1)

            def step(i, h):
                lift(i, h)
                if later(i) or h:
                    pieces(*before(i, h))

            block_rounds(dve, step)
            pieces(NB // 2, 0)

        @block.tensor
        def _(pe):
            pe.wait_ge(weights, 16)

            def turn(i, h):
                pe.wait_ge(taken[h], i + 1)
                if later(i):
                    pe.wait_ge(lifted[h], i)
                nc.tensor.transpose(c.bank[h][:, 0:P], xb[:, h, :], c.ident[:, :]).then_inc(turned[h], 1)

            def products(i, h):
                pe.wait_ge(lifted[h], i + 1)
                for j in range(PIECES):
                    if later(i) or h or j >= RING:
                        ago = h * PIECES + j - RING
                        pe.wait_ge((even, odd)[ago % 2], i * (2 * HP) + ago // 2 + 1)
                    nc.tensor.matmul(c.bank[2 + j % RING][:, 0:PW], xT[:, h, :], wf[:, j * PW:(j + 1) * PW],
                                     start=True, stop=True).then_inc(made, 1)

            def step(i, h):
                turn(i, h)
                if later(i) or h:
                    products(*before(i, h))

            block_rounds(pe, step)
            products(NB // 2, 0)


def vector_steps(c, name, work):
    with c.stage(name, "step") as (block, stepped):
        @block.vector
        def _(dve):
            o = Order(dve, stepped)
            work(c.nc.vector, o.link)


def load(c, name, *pairs):
    with c.stage(name, "moved") as (block, moved):
        @block.sync
        def _(sp):
            for dst, src in pairs:
                sp.dma_start(dst, src).then_inc(moved, 16)
            sp.wait_ge(moved, 16 * len(pairs))


def over(vec, n):
    return vec.rearrange("p (a w) -> p a w", a=1).to_broadcast([P, n, vec.shape[-1]])


def inner(col, w):
    return col.rearrange("p (n a) -> p n a", a=1).to_broadcast([P, col.shape[-1], w])


def layer_norm(c, name, x, h, eps=1e-5):
    nc = c.nc
    with (nc.sbuf_tensor(f"{name}_sq", [P, NB, D], fp32) as sq,
          nc.sbuf_tensor(f"{name}_sum", [P, NB], fp32) as total,
          nc.sbuf_tensor(f"{name}_mean", [P, NB], fp32) as mean,
          nc.sbuf_tensor(f"{name}_sd", [P, NB], fp32) as sd,
          c.stage(name, "step", "var", "root") as (block, stepped, var, root)):
        @block.vector
        def _(dve):
            v = nc.vector
            o = Order(dve, stepped)
            X = x[:, 0:NB, :]
            o.link(v.tensor_tensor(X, X, h, ALU.add))
            o.link(v.tensor_reduce(total[:, :], X, AX.X, ALU.add))
            o.link(v.tensor_scalar(mean[:, :], total[:, :], 1.0 / D, None, ALU.mult))
            o.link(v.tensor_tensor(X, X, inner(mean[:, :], D), ALU.subtract))
            o.link(v.tensor_tensor(sq[:, :, :], X, X, ALU.mult))
            o.link(v.tensor_reduce(total[:, :], sq[:, :, :], AX.X, ALU.add))
            v.tensor_scalar(total[:, :], total[:, :], 1.0 / D, float(eps), ALU.mult, ALU.add).then_inc(var, 1)
            dve.wait_ge(root, 1)
            o.link(v.reciprocal(sd[:, :], sd[:, :]))
            o.link(v.tensor_tensor(X, X, inner(sd[:, :], D), ALU.mult))

        @block.scalar
        def _(act):
            act.wait_ge(var, 1)
            nc.scalar.activation(sd[:, :], total[:, :], ACT.Sqrt).then_inc(root, 1)


def gat_max(c, name, table, edges, best):
    nc = c.nc
    G2 = 2 * GRP
    with (nc.sbuf_tensor(f"{name}_G", [P, 2, GRP, 2], fp32) as G,
          nc.sbuf_tensor(f"{name}_ib", [P, 2, GRP], i32) as ib,
          nc.sbuf_tensor(f"{name}_other", [P, 2, GRP, P], fp32) as other,
          nc.sbuf_tensor(f"{name}_alpha", [P, 2, G2, P], fp32) as alpha,
          nc.sbuf_tensor(f"{name}_top", [P, 2, G2], fp32) as top,
          c.stage(name, "gathered0", "gathered1", "copied", "started", "marked0", "marked1", "shifted0",
                  "shifted1", "turned0", "turned1", "maxed") as (
                      block, gathered0, gathered1, copied, started, marked0, marked1, shifted0, shifted1,
                      turned0, turned1, maxed)):
        gathered, marked = (gathered0, gathered1), (marked0, marked1)
        shifted, turned = (shifted0, shifted1), (turned0, turned1)

        @block.gpsimd
        def _(pool):
            gather_groups(nc, pool, table, edges.node, ib, G, gathered, shifted, copied, started)

        @block.vector
        def _(dve):
            def mark(i, h):
                if later(i):
                    dve.wait_ge(shifted[h], i)
                for k in range(GRP):
                    at = bass.ds(i * G2 + (h * GRP + k), 1)
                    last = nc.vector.tensor_scalar(other[:, h, k, :], c.iota[:, :], edges.local[:, at], NEG,
                                                   ALU.not_equal, ALU.mult)
                last.then_inc(marked[h], 1)

            def reduce(i, h):
                b = chunk_blocks(dve, edges.block, i * 2 + h)
                dve.wait_ge(turned[h], i + 1)
                o = Order(dve, maxed, i * (2 * (GRP + 1)) + h * (GRP + 1))
                for q in range(4):
                    last = nc.vector.tensor_reduce(top[:, h, 4 * q:4 * q + 4],
                                                   c.bank[4 * h + q][:, :].rearrange("p (k e) -> p k e", e=P),
                                                   AX.X, ALU.max)
                o.link(last)
                for k in range(GRP):
                    o.link(nc.vector.tensor_tensor(best[:, bass.ds(b[k], 1), :], best[:, bass.ds(b[k], 1), :],
                                                   top[:, h, 2 * k:2 * k + 2].rearrange("p (a w) -> p a w", a=1),
                                                   ALU.max))

            def step(i, h, ni, nh):
                if ni is not None:
                    mark(ni, nh)
                reduce(i, h)

            mark(0, 0)
            pipeline(dve, step)

        @block.scalar
        def _(act):
            def shift(i):
                for h in range(2):
                    act.wait_ge(marked[h], i + 1)
                    act.wait_ge(gathered[h], i * (16 * GRP) + 16 * GRP)
                    if later(i):
                        act.wait_ge(turned[h], i)
                    for k in range(GRP):
                        for d in range(2):
                            last = nc.scalar.activation(alpha[:, h, 2 * k + d, :], other[:, h, k, :], ACT.Identity,
                                                        bias=G[:, h, k, d:d + 1])
                    last.then_inc(shifted[h], 1)

            rounds(act, PAIRS, shift)

        @block.tensor
        def _(pe):
            def turn(i):
                for h in range(2):
                    pe.wait_ge(shifted[h], i + 1)
                    if later(i):
                        pe.wait_ge(maxed, i * (2 * (GRP + 1)) - (GRP + 1) * (2 - h) + 1)
                    for k in range(G2):
                        at = (k % 4) * P
                        last = nc.tensor.transpose(c.bank[4 * h + k // 4][:, at:at + P], alpha[:, h, k, :],
                                                   c.ident[:, :])
                    last.then_inc(turned[h], 1)

            rounds(pe, PAIRS, turn)


def gat_pass(c, name, table, edges, node, acc):
    nc = c.nc
    with ExitStack() as s:
        def sb(n, shape, dt):
            return s.enter_context(nc.sbuf_tensor(f"{name}_{n}", shape, dt))

        G = sb("G", [P, 2, GRP, GW], fp32)
        ib = sb("ib", [P, 2, GRP], i32)
        onehot = sb("onehot", [P, 2, GRP, P], bf16)
        onehotT = sb("onehotT", [P, 2, GRP, P], fp32)
        wone = sb("weighted", [P, 2, GRP, 2, P], fp32)
        logit = sb("logit", [P, 2, GRP, 2], fp32)
        leaky = sb("leaky", [P, 2, GRP, 2], fp32)
        e = sb("exp", [P, 2, GRP, 2], fp32)
        names = [n + d for n in ("gathered", "used", "marked", "turned", "spread", "looked", "ready", "exped",
                                 "weighv", "weigha") for d in "01"]
        block, *sems = s.enter_context(c.stage(name, *names, "copied", "started", "added", "logits"))
        gathered, used, marked, turned, spread, looked, ready, exped, weighv, weigha = (
            tuple(sems[2 * n:2 * n + 2]) for n in range(10))
        copied, started, added, logits = sems[20:]

        def sums(h, k):
            return c.bank[3 * h + k // 3][:, (k % 3) * 2 * HW:(k % 3 + 1) * 2 * HW]

        nodeof = c.bank[7][:, 0:2 * GRP * 4].rearrange("p (h k w) -> p h k w", h=2, w=4)
        turnbank = c.bank[6][:, :].bitcast(bf16)

        @block.gpsimd
        def _(pool):
            gather_groups(nc, pool, table, edges.node, ib, G, gathered, used, copied, started)

        @block.vector
        def _(dve):
            def mark(i, h):
                if later(i):
                    dve.wait_ge(weigha[h], i)
                for k in range(GRP):
                    at = bass.ds(i * (2 * GRP) + (h * GRP + k), 1)
                    last = nc.vector.tensor_scalar(onehot[:, h, k, :], c.iota[:, :], edges.local[:, at], None,
                                                   ALU.is_equal)
                last.then_inc(marked[h], 1)

            def logit_of(i, h):
                dve.wait_ge(gathered[h], i * (16 * GRP) + 16 * GRP)
                dve.wait_ge(looked[h], i + 1)
                o = Order(dve, logits, i * 6 + h * 3)
                o.link(nc.vector.tensor_tensor(logit[:, h, :, :], G[:, h, :, 2 * HW:GW], nodeof[:, h, :, 0:2], ALU.add))
                o.link(nc.vector.scalar_tensor_tensor(leaky[:, h, :, :], logit[:, h, :, :], 0.2, logit[:, h, :, :],
                                                      ALU.mult, ALU.max))
                o.link(nc.vector.tensor_tensor(leaky[:, h, :, :], leaky[:, h, :, :], nodeof[:, h, :, 2:4],
                                               ALU.subtract))
                nc.vector.tensor_scalar(logit[:, h, :, :], leaky[:, h, :, :], 0.0, None, ALU.min).then_inc(ready[h], 1)

            def weigh(i, h):
                dve.wait_ge(exped[h], i + 1)
                if later(i):
                    dve.wait_ge(used[h], i)
                for k in range(GRP):
                    at = bass.ds(i * (2 * GRP) + (h * GRP + k), 1)
                    last = nc.vector.tensor_scalar(wone[:, h, k, 0, :], c.iota[:, :], edges.local[:, at],
                                                   e[:, h, k, 0:1], ALU.is_equal, ALU.mult)
                last.then_inc(weighv[h], 1)

            def add(i, h):
                b = chunk_blocks(dve, edges.block, i * 2 + h)
                dve.wait_ge(used[h], i + 1)
                o = Order(dve, added, i * (2 * GRP) + h * GRP)
                for k in range(GRP):
                    o.link(nc.vector.tensor_tensor(acc[:, bass.ds(b[k], 1), :], acc[:, bass.ds(b[k], 1), :],
                                                   sums(h, k).rearrange("p (a w) -> p a w", a=1), ALU.add))

            def step(i, h, ni, nh):
                if ni is not None:
                    mark(ni, nh)
                logit_of(i, h)
                if later(i) or h:
                    add(*before(i, h))
                weigh(i, h)

            mark(0, 0)
            pipeline(dve, step, add)

        @block.scalar
        def _(act):
            def spread_out(i, h):
                act.wait_ge(turned[h], i + 1)
                if later(i):
                    act.wait_ge(looked[h], i)
                nc.scalar.activation(onehotT[:, h, :, :].rearrange("p k n -> p (k n)"), turnbank,
                                     ACT.Copy).then_inc(spread[h], 1)

            def weigh(i, h):
                act.wait_ge(ready[h], i + 1)
                if later(i):
                    act.wait_ge(weighv[h], i)
                    act.wait_ge(weigha[h], i)
                nc.scalar.activation(e[:, h, :, :], logit[:, h, :, :], ACT.Exp).then_inc(exped[h], 1)
                act.wait_ge(exped[h], i + 1)
                if later(i):
                    act.wait_ge(used[h], i)
                for k in range(GRP):
                    last = nc.scalar.activation(wone[:, h, k, 1, :], onehot[:, h, k, :], ACT.Copy,
                                                scale=e[:, h, k, 1:2])
                last.then_inc(weigha[h], 1)

            def step(i, h, ni, nh):
                weigh(i, h)
                if ni is not None:
                    spread_out(ni, nh)

            spread_out(0, 0)
            pipeline(act, step)

        @block.tensor
        def _(pe):
            def turn(i, h):
                pe.wait_ge(marked[h], i + 1)
                if later(i) or h:
                    bi, bh = before(i, h)
                    pe.wait_ge(spread[bh], bi + 1)
                for k in range(GRP):
                    last = nc.tensor.transpose(turnbank[:, k * P:(k + 1) * P], onehot[:, h, k, :], c.identb[:, :])
                last.then_inc(turned[h], 1)

            def look(i, h):
                b = chunk_blocks(pe, edges.block, i * 2 + h)
                pe.wait_ge(spread[h], i + 1)
                if later(i):
                    pe.wait_ge(ready[h], i)
                for k in range(GRP):
                    last = nc.tensor.matmul(nodeof[:, h, k, :], onehotT[:, h, k, :],
                                            node[:, bass.ds(b[k], 1), :].rearrange("p a w -> p (a w)"),
                                            start=True, stop=True)
                last.then_inc(looked[h], 1)

            def total(i, h):
                pe.wait_ge(weighv[h], i + 1)
                pe.wait_ge(weigha[h], i + 1)
                pe.wait_ge(gathered[h], i * (16 * GRP) + 16 * GRP)
                if later(i):
                    pe.wait_ge(added, i * (2 * GRP) - GRP + h * GRP)
                for k in range(GRP):
                    for d in range(2):
                        last = nc.tensor.matmul(sums(h, k)[:, d * HW:(d + 1) * HW], wone[:, h, k, d, :],
                                                G[:, h, k, d * HW:(d + 1) * HW], start=True, stop=True)
                last.then_inc(used[h], 1)

            def step(i, h, ni, nh):
                if ni is not None:
                    turn(ni, nh)
                total(i, h)
                if ni is not None:
                    look(ni, nh)

            turn(0, 0)
            look(0, 0)
            pipeline(pe, step)


def by_node(table):
    return table.rearrange("(b p) w -> p b w", p=P)


def rgcn(c, x, edges, W, root, bias, res_W, res_b, ytab, out):
    nc = c.nc
    h = x
    for l in range(2):
        relation_table(c, f"rtable{l}", h, W[l], ytab)
        with (nc.sbuf_tensor(f"rg_acc{l}", [P, KEYS, D], fp32) as acc,):
            vector_steps(c, f"rclear{l}", lambda v, link: link(v.memset(acc[:, :, :], 0.0)))
            edge_pass(c, f"rpass{l}", ytab.rearrange("n (r k) -> (n r) k", k=D), edges.row, edges, acc, weighted=True)
            with (nc.sbuf_tensor(f"rg_w{l}", [D, 2 * D], fp32) as w,
                  nc.sbuf_tensor(f"rg_b{l}", [P, 2 * D], fp32) as b,
                  nc.sbuf_tensor(f"rg_t{l}", [P, NB, 2 * D], fp32) as t):
                load(c, f"rload{l}", (w[:, 0:D], root[l]), (w[:, D:2 * D], res_W[l]),
                     (b[:, 0:D], bias[l:l + 1, :].to_broadcast([P, D])),
                     (b[:, D:2 * D], res_b[l:l + 1, :].to_broadcast([P, D])))
                node_product(c, f"rroot{l}", h, w[:, :], t)

                def combine(v, link):
                    link(v.tensor_tensor(t[:, :, :], t[:, :, :], over(b[:, :], NB), ALU.add))
                    link(v.tensor_tensor(t[:, :, 0:D], t[:, :, 0:D], acc[:, 0:NB, :], ALU.add))
                    link(v.tensor_scalar(t[:, :, :], t[:, :, :], 0.0, None, ALU.max))
                    link(v.tensor_tensor(out[:, :, :], t[:, :, 0:D], t[:, :, D:2 * D], ALU.add))

                vector_steps(c, f"rsum{l}", combine)
        h = out


def gin(c, x, edges, W1, b1, W2, b2, gamma, beta, xtab, out, eps=1e-5):
    nc = c.nc
    load(c, "gintab", (by_node(xtab), x[:, :, :]))
    with (nc.sbuf_tensor("gi_acc", [P, KEYS, D], fp32) as acc,
          nc.sbuf_tensor("gi_w", [D, 2 * D], fp32) as w,
          nc.sbuf_tensor("gi_v", [P, 4, D], fp32) as vec,
          nc.sbuf_tensor("gi_m", [P, 4, D], fp32) as m,
          nc.sbuf_tensor("gi_sq", [P, NB, D], fp32) as sq):
        load(c, "ginload", (w[:, 0:D], W1), (w[:, D:2 * D], W2),
             *((vec[:, n, :], a.rearrange("(a w) -> a w", a=1).to_broadcast([P, D]))
               for n, a in enumerate((b1, b2, gamma, beta))))

        def begin(v, link):
            link(v.memset(acc[:, NB:KEYS, :], 0.0))
            link(v.tensor_copy(acc[:, 0:NB, :], x[:, :, :]))

        vector_steps(c, "ginbegin", begin)
        edge_pass(c, "ginpass", xtab, edges.node, edges, acc)
        for n, src in ((0, acc), (1, out)):
            node_product(c, f"gin{n}", src, w[:, n * D:(n + 1) * D], out)

            def bias_relu(v, link):
                link(v.tensor_tensor(out[:, :, :], out[:, :, :], over(vec[:, n, :], NB), ALU.add))
                link(v.tensor_scalar(out[:, :, :], out[:, :, :], 0.0, None, ALU.max))

            vector_steps(c, f"ginrelu{n}", bias_relu)
        with c.stage("ginnorm", "step", "part", "whole", "var", "root") as (block, stepped, part, whole, var, sqrt):
            @block.vector
            def _(dve):
                v = nc.vector
                o = Order(dve, stepped)
                o.link(v.tensor_scalar(out[:, NB - 1, :], out[:, NB - 1, :], c.valid[:, 0:1], None, ALU.mult))
                v.tensor_reduce(m[:, 0, :], out[:, :, :].rearrange("p b d -> p d b"), AX.X, ALU.add).then_inc(part, 1)
                dve.wait_ge(whole, 1)
                o.link(v.tensor_scalar(m[:, 1, :], c.bank[0][:, 0:D], 1.0 / N, None, ALU.mult))
                o.link(v.tensor_tensor(out[:, :, :], out[:, :, :], over(m[:, 1, :], NB), ALU.subtract))
                o.link(v.tensor_scalar(out[:, NB - 1, :], out[:, NB - 1, :], c.valid[:, 0:1], None, ALU.mult))
                o.link(v.tensor_tensor(sq[:, :, :], out[:, :, :], out[:, :, :], ALU.mult))
                v.tensor_reduce(m[:, 2, :], sq[:, :, :].rearrange("p b d -> p d b"), AX.X, ALU.add).then_inc(part, 1)
                dve.wait_ge(whole, 2)
                v.tensor_scalar(m[:, 3, :], c.bank[1][:, 0:D], 1.0 / N, float(eps), ALU.mult, ALU.add).then_inc(var, 1)
                dve.wait_ge(sqrt, 1)
                o.link(v.reciprocal(m[:, 0, :], m[:, 0, :]))
                o.link(v.tensor_tensor(m[:, 0, :], m[:, 0, :], vec[:, 2, :], ALU.mult))
                o.link(v.tensor_tensor(out[:, :, :], out[:, :, :], over(m[:, 0, :], NB), ALU.mult))
                o.link(v.tensor_tensor(out[:, :, :], out[:, :, :], over(vec[:, 3, :], NB), ALU.add))

            @block.tensor
            def _(pe):
                for n in range(2):
                    pe.wait_ge(part, n + 1)
                    nc.tensor.matmul(c.bank[n][:, 0:D], c.ones[:, :], m[:, 2 * n, :], start=True,
                                     stop=True).then_inc(whole, 1)

            @block.scalar
            def _(act):
                act.wait_ge(var, 1)
                nc.scalar.activation(m[:, 0, :], m[:, 3, :], ACT.Sqrt).then_inc(sqrt, 1)


def gat_layer(c, name, src, W, a_s, a_d, edges, gtab, atab, acc):
    nc = c.nc
    with (nc.sbuf_tensor(f"{name}_node", [P, KEYS, 4], fp32) as node,
          nc.sbuf_tensor(f"{name}_alpha", [P, NB, 4], fp32) as alpha,
          nc.sbuf_tensor(f"{name}_best", [P, KEYS, 2], fp32) as best,
          nc.sbuf_tensor(f"{name}_self", [P, NB, 2], fp32) as self_e,
          nc.sbuf_tensor(f"{name}_self2", [P, NB, 2], fp32) as self_l,
          nc.sbuf_tensor(f"{name}_tab", [P, NB, GW], fp32) as tab):
        with (nc.sbuf_tensor(f"{name}_w", [src.shape[-1], 2 * D], fp32) as w,
              nc.sbuf_tensor(f"{name}_a", [P, 4 * D], fp32) as av,
              nc.sbuf_tensor(f"{name}_h", [P, NB, 2 * D], fp32) as h):
            prod = acc[:, 0:NB, 0:2 * D]
            load(c, f"{name}load", (w[:, :], W),
                 *((av[:, (2 * n + d) * D:(2 * n + d + 1) * D], a[d:d + 1, :].to_broadcast([P, D]))
                   for n, a in enumerate((a_s, a_d)) for d in range(2)))
            node_product(c, f"{name}h", src, w[:, :], h)

            def prepare(v, link):
                for n in range(2):
                    link(v.tensor_tensor(prod, h[:, :, :], over(av[:, 2 * n * D:2 * (n + 1) * D], NB), ALU.mult))
                    for d in range(2):
                        link(v.tensor_reduce(alpha[:, :, 2 * n + d], prod[:, :, d * D:(d + 1) * D], AX.X, ALU.add))
                for d in range(2):
                    link(v.tensor_copy(tab[:, :, d * HW:d * HW + D], h[:, :, d * D:(d + 1) * D]))
                    link(v.memset(tab[:, :, d * HW + D:d * HW + D + 1], 1.0))
                link(v.tensor_copy(tab[:, :, 2 * HW:GW], alpha[:, :, 0:2]))
                link(v.memset(best[:, :, :], 0.0))
                link(v.tensor_copy(best[:, 0:NB, :], alpha[:, :, 0:2]))

            vector_steps(c, f"{name}prep", prepare)
        load(c, f"{name}tables", (by_node(gtab), tab[:, :, :]), (by_node(atab), alpha[:, :, 0:2]))
        gat_max(c, f"{name}max", atab, edges, best)
        with c.stage(f"{name}own", "step", "ready", "exped") as (block, stepped, ready, exped):
            @block.vector
            def _(dve):
                v = nc.vector
                o = Order(dve, stepped)
                o.link(v.memset(node[:, :, :], 0.0))
                o.link(v.tensor_copy(node[:, 0:NB, 0:2], alpha[:, :, 2:4]))
                o.link(v.tensor_tensor(best[:, 0:NB, :], best[:, 0:NB, :], alpha[:, :, 2:4], ALU.add))
                o.link(v.scalar_tensor_tensor(node[:, 0:NB, 2:4], best[:, 0:NB, :], 0.2, best[:, 0:NB, :],
                                              ALU.mult, ALU.max))
                o.link(v.tensor_tensor(self_l[:, :, :], alpha[:, :, 0:2], alpha[:, :, 2:4], ALU.add))
                o.link(v.scalar_tensor_tensor(self_e[:, :, :], self_l[:, :, :], 0.2, self_l[:, :, :], ALU.mult, ALU.max))
                v.tensor_tensor(self_l[:, :, :], self_e[:, :, :], node[:, 0:NB, 2:4], ALU.subtract).then_inc(ready, 1)
                dve.wait_ge(exped, 1)
                o.link(v.memset(acc[:, NB:KEYS, :], 0.0))
                for d in range(2):
                    o.link(v.tensor_tensor(acc[:, 0:NB, d * HW:(d + 1) * HW], tab[:, :, d * HW:(d + 1) * HW],
                                           self_e[:, :, d:d + 1].to_broadcast([P, NB, HW]), ALU.mult))

            @block.scalar
            def _(act):
                act.wait_ge(ready, 1)
                nc.scalar.activation(self_e[:, :, :], self_l[:, :, :], ACT.Exp).then_inc(exped, 1)
        gat_pass(c, f"{name}pass", gtab, edges, node, acc)

        def divide(v, link):
            for d in range(2):
                link(v.reciprocal(self_e[:, :, d:d + 1], acc[:, 0:NB, d * HW + D:(d + 1) * HW]))
                link(v.tensor_tensor(acc[:, 0:NB, d * HW:d * HW + D], acc[:, 0:NB, d * HW:d * HW + D],
                                     self_e[:, :, d:d + 1].to_broadcast([P, NB, D]), ALU.mult))

        vector_steps(c, f"{name}div", divide)


def gat(c, x, edges, W1, as1, ad1, b1, W2, as2, ad2, b2, gtab, atab, out):
    nc = c.nc
    with (nc.sbuf_tensor("gat_bias", [P, 3 * D], fp32) as bias,
          nc.sbuf_tensor("gat_acc", [P, KEYS, 2 * HW], fp32) as acc):
        load(c, "gatbias", (bias[:, 0:2 * D], b1.rearrange("(a w) -> a w", a=1).to_broadcast([P, 2 * D])),
             (bias[:, 2 * D:3 * D], b2.rearrange("(a w) -> a w", a=1).to_broadcast([P, D])))
        gat_layer(c, "gata", x, W1, as1, ad1, edges, gtab, atab, acc)
        with nc.sbuf_tensor("gat_h", [P, NB, 2 * D], fp32) as h:
            def concat(v, link):
                for d in range(2):
                    link(v.tensor_tensor(h[:, :, d * D:(d + 1) * D], acc[:, 0:NB, d * HW:d * HW + D],
                                         over(bias[:, d * D:(d + 1) * D], NB), ALU.add))

            vector_steps(c, "gatcat", concat)
            gat_layer(c, "gatb", h, W2, as2, ad2, edges, gtab, atab, acc)

        def mean(v, link):
            link(v.tensor_tensor(out[:, :, :], acc[:, 0:NB, 0:D], acc[:, 0:NB, HW:HW + D], ALU.add))
            link(v.tensor_scalar(out[:, :, :], out[:, :, :], 0.5, None, ALU.mult))
            link(v.tensor_tensor(out[:, :, :], out[:, :, :], over(bias[:, 2 * D:3 * D], NB), ALU.add))

        vector_steps(c, "gatmean", mean)


def sage(c, x, edges, W1_l, b1, W1_r, W2_l, b2, W2_r, invdeg, xtab, out):
    nc = c.nc
    with (nc.sbuf_tensor("sg_acc", [P, KEYS, D], fp32) as acc,
          nc.sbuf_tensor("sg_w1", [2 * D, 2 * D], fp32) as w1,
          nc.sbuf_tensor("sg_w2", [2 * D, 2 * D], fp32) as w2,
          nc.sbuf_tensor("sg_b", [P, 3 * D], fp32) as b,
          nc.sbuf_tensor("sg_in", [P, NB, 2 * D], fp32) as both,
          nc.sbuf_tensor("sg_h", [P, NB, 2 * D], fp32) as h):
        load(c, "sageload", (by_node(xtab), x[:, :, :]), (w1[0:D, :], W1_l), (w1[D:2 * D, :], W1_r),
             (w2[:, 0:D], W2_l), (w2[:, D:2 * D], W2_r),
             (b[:, 0:2 * D], b1.rearrange("(a w) -> a w", a=1).to_broadcast([P, 2 * D])),
             (b[:, 2 * D:3 * D], b2.rearrange("(a w) -> a w", a=1).to_broadcast([P, D])))
        vector_steps(c, "sageclear0", lambda v, link: link(v.memset(acc[:, :, :], 0.0)))
        edge_pass(c, "sagepass0", xtab, edges.node, edges, acc)

        def mean_and_own(v, link):
            link(v.tensor_tensor(both[:, :, 0:D], acc[:, 0:NB, :], inner(invdeg[:, :], D), ALU.mult))
            link(v.tensor_copy(both[:, :, D:2 * D], x[:, :, :]))

        vector_steps(c, "sagemean", mean_and_own)
        node_product(c, "sage0", both, w1[:, :], h)

        def relu(v, link):
            link(v.tensor_tensor(h[:, :, :], h[:, :, :], over(b[:, 0:2 * D], NB), ALU.add))
            link(v.tensor_scalar(h[:, :, :], h[:, :, :], 0.0, None, ALU.max))

        vector_steps(c, "sagerelu", relu)
        node_product(c, "sage1", h, w2[:, :], both)
        load(c, "sagetab", (by_node(xtab), both[:, :, 0:D]))
        vector_steps(c, "sageclear1", lambda v, link: link(v.memset(acc[:, :, :], 0.0)))
        edge_pass(c, "sagepass1", xtab, edges.node, edges, acc)

        def total(v, link):
            link(v.tensor_tensor(out[:, :, :], acc[:, 0:NB, :], inner(invdeg[:, :], D), ALU.mult))
            link(v.tensor_tensor(out[:, :, :], out[:, :, :], both[:, :, D:2 * D], ALU.add))
            link(v.tensor_tensor(out[:, :, :], out[:, :, :], over(b[:, 2 * D:3 * D], NB), ALU.add))

        vector_steps(c, "sagesum", total)


def program(nc, x, src, dst, relation, L0_W, L0_root, L0_bias, L0_res_W, L0_res_b, L1_W1, L1_b1, L1_W2, L1_b2,
            L1_gamma, L1_beta, L2_W1, L2_as1, L2_ad1, L2_b1, L2_W2, L2_as2, L2_ad2, L2_b2, L3_W1_l, L3_b1,
            L3_W1_r, L3_W2_l, L3_b2, L3_W2_r, out):
    ctx = ExitStack()
    with ctx:
        def dram(name, shape, dt):
            return nc.dram_tensor(name, shape, dt, kind="Internal").ap()

        c = Chip(nc, ctx)
        listed = dram("edges_sorted", [P + 1, CH * 4], i32)
        chunk_block = dram("chunk_block", [CH], i32)
        ytab = dram("relation_products", [NB * P, R * D], fp32)
        xtab = dram("node_rows", [NB * P, D], fp32)
        gtab = dram("gat_rows", [NB * P, GW], fp32)
        atab = dram("alpha_rows", [NB * P, 2], fp32)
        constants(c)
        X = c.keep("x", [P, NB, D], fp32)
        H = c.keep("h", [P, NB, D], fp32)
        invdeg = c.keep("invdeg", [P, NB], fp32)
        to_dst = Edges(c, "to_dst", typed=True)
        to_src = Edges(c, "to_src", typed=False)
        sort_edges(c, "sortd", dst, src, relation, listed[0:P, :], chunk_block, to_dst)
        sort_edges(c, "sorts", src, dst, None, listed[0:P, :], chunk_block, to_src)
        with nc.sbuf_tensor("counts", [P, KEYS, R], fp32) as counts:
            relation_weights(c, to_dst, counts)

            def degrees(v, link):
                link(v.tensor_reduce(invdeg[:, :], counts[:, 0:NB, :], AX.X, ALU.add))
                link(v.tensor_scalar(invdeg[:, :], invdeg[:, :], 1.0, None, ALU.max))
                link(v.reciprocal(invdeg[:, :], invdeg[:, :]))
                link(v.memset(X[:, NB - 1, :], 0.0))

            vector_steps(c, "degrees", degrees)
        load(c, "loadx", (X[:, 0:NB - 1, :], x[0:(NB - 1) * P, :].rearrange("(b p) d -> p b d", p=P)),
             (X[0:LAST, NB - 1, :], x[(NB - 1) * P:N, :]))
        rgcn(c, X, to_dst, L0_W, L0_root, L0_bias, L0_res_W, L0_res_b, ytab, H)
        layer_norm(c, "norm0", X, H[:, :, :])
        gin(c, X, to_src, L1_W1, L1_b1, L1_W2, L1_b2, L1_gamma, L1_beta, xtab, H)
        layer_norm(c, "norm1", X, H[:, :, :])
        gat(c, X, to_dst, L2_W1, L2_as1, L2_ad1, L2_b1, L2_W2, L2_as2, L2_ad2, L2_b2, gtab, atab, H)
        layer_norm(c, "norm2", X, H[:, :, :])
        sage(c, X, to_dst, L3_W1_l, L3_b1, L3_W1_r, L3_W2_l, L3_b2, L3_W2_r, invdeg, xtab, H)
        layer_norm(c, "norm3", X, H[:, :, :])
        load(c, "store", (out[0:(NB - 1) * P, :].rearrange("(b p) d -> p b d", p=P), X[:, 0:NB - 1, :]),
             (out[(NB - 1) * P:N, :], X[0:LAST, NB - 1, :]))


INPUTS = ["x", "src", "dst", "edge_type_65", "L0_gnn_W", "L0_gnn_root", "L0_gnn_bias", "L0_gnn_res_W",
          "L0_gnn_res_b", "L1_gnn_W1", "L1_gnn_b1", "L1_gnn_W2", "L1_gnn_b2", "L1_gnn_gamma", "L1_gnn_beta",
          "L2_gnn_W1", "L2_gnn_as1", "L2_gnn_ad1", "L2_gnn_b1", "L2_gnn_W2", "L2_gnn_as2", "L2_gnn_ad2",
          "L2_gnn_b2", "L3_gnn_W1_l", "L3_gnn_b1", "L3_gnn_W1_r", "L3_gnn_W2_l", "L3_gnn_b2", "L3_gnn_W2_r"]


def kernel(**inputs):
    import numpy as np
    import concourse.bacc as bacc
    from concourse import mybir as mb
    from concourse.bass_utils import run_bass_kernel_spmd

    nc = bacc.Bacc("TRN2", target_bir_lowering=False, num_devices=1)
    arrays, args = {}, []
    for name in INPUTS:
        a = np.ascontiguousarray(inputs[name])
        arrays[f"in_{name}"] = a
        args.append(nc.dram_tensor(f"in_{name}", a.shape, mb.dt.from_np(a.dtype), kind="ExternalInput").ap())
    args.append(nc.dram_tensor("out_x", (N, D), mb.dt.float32, kind="ExternalOutput").ap())
    program(nc, *args)
    r = run_bass_kernel_spmd(nc, [arrays], core_ids=[0])
    return r.results[0]["out_x"]
```

```python
import concourse.bass as bass
from concourse import mybir
from contextlib import ExitStack, contextmanager

P = 128
N = 6250
E = 206250
D = 64
R = 65
NB = -(-N // P)
LAST = N - (NB - 1) * P
PADNODE = NB * P
KEYS = NB + 1
EC = -(-E // P)
ETAIL = E - (P - 1) * EC
UNIT = 2
USHIFT = 8
GRP = 8
GU = GRP // UNIT
PAIRS = -(-(-(-EC // UNIT) + KEYS) // (2 * GU))
UNITS = PAIRS * 2 * GU
CH = UNITS * UNIT
UP = -(-UNITS // P)
NTAB = KEYS * P
HW = D + 1
GW = 2 * HW + 2
NEG = -3.0e38
SC = 13
assert EC % (2 * SC) == 0 and UNIT * P == 1 << USHIFT

fp32, bf16, i32 = mybir.dt.float32, mybir.dt.bfloat16, mybir.dt.int32
ALU = mybir.AluOpType
ACT = mybir.ActivationFunctionType
AX = mybir.AxisListType


def later(i):
    return not (isinstance(i, int) and i == 0)


def rounds(eng, n, body):
    body(0)
    with eng.Fori(1, n) as i:
        body(i)


class Order:

    def __init__(self, eng, sem, base=0):
        self.eng, self.sem, self.base, self.n = eng, sem, base, 0

    def link(self, ins):
        self.n += 1
        ins.then_inc(self.sem, 1)
        self.eng.wait_ge(self.sem, self.base + self.n)


class Chip:

    def __init__(self, nc, ctx):
        self.nc, self.ctx = nc, ctx
        self.stages = 0
        self.block = self.buffers = None
        self.bank = [ctx.enter_context(nc.psum_tensor(f"bank{i}", [P, 512], fp32)) for i in range(8)]

    def keep(self, name, shape, dt):
        return self.ctx.enter_context(self.nc.sbuf_tensor(name, shape, dt))

    @contextmanager
    def together(self):
        with ExitStack() as buffers:
            self.handles, self.buffers = [], buffers
            with self.nc.Block() as block:
                self.block = block
                yield
            self.clear(self.handles)
            self.block = self.buffers = None

    def clear(self, handles):
        self.nc.clear_and_free_semaphores(handles)
        self.nc.all_engine_barrier(sem_only=True)

    @contextmanager
    def stage(self, name, *sems):
        self.stages += 1
        handles = [self.nc.alloc_semaphore(f"{name}{self.stages}_{s}") for s in sems]
        if self.block is not None:
            self.handles += handles
            yield (self.block, *handles)
            return
        with self.nc.Block() as block:
            yield (block, *handles)
        self.clear(handles)

    @contextmanager
    def scope(self):
        with ExitStack() as own:
            buffers = self.buffers if self.buffers is not None else own
            yield lambda name, shape, dt: buffers.enter_context(self.nc.sbuf_tensor(name, shape, dt))


def constants(c):
    nc = c.nc
    c.iota = c.keep("iota", [P, P], fp32)
    c.keyno = c.keep("keyno", [P, KEYS], fp32)
    c.ident = c.keep("ident", [P, P], fp32)
    c.identb = c.keep("identb", [P, P], bf16)
    c.ones = c.keep("ones", [P, P], fp32)
    c.lower = c.keep("lower", [P, P], fp32)
    c.unitno = c.keep("unitno", [P, UP], fp32)
    c.rowno = c.keep("rowno", [P, 1], fp32)
    c.valid = c.keep("valid", [P, 1], fp32)
    with c.stage("const", "made", "step") as (block, made, step):
        @block.gpsimd
        def _(pool):
            nc.gpsimd.iota(c.iota[:, :], pattern=[[1, P]], base=0, channel_multiplier=0,
                           allow_small_or_imprecise_dtypes=True).then_inc(made, 1)
            nc.gpsimd.iota(c.keyno[:, :], pattern=[[1, KEYS]], base=0, channel_multiplier=0,
                           allow_small_or_imprecise_dtypes=True).then_inc(made, 1)
            nc.gpsimd.iota(c.unitno[:, :], pattern=[[1, UP]], base=0, channel_multiplier=UP,
                           allow_small_or_imprecise_dtypes=True).then_inc(made, 1)
            nc.gpsimd.iota(c.rowno[:, :], pattern=[[1, 1]], base=0, channel_multiplier=1,
                           allow_small_or_imprecise_dtypes=True).then_inc(made, 1)
            nc.gpsimd.memset(c.ones[:, :], 1.0).then_inc(made, 1)

        @block.vector
        def _(dve):
            dve.wait_ge(made, 5)
            nc.vector.tensor_scalar(c.ident[:, :], c.iota[:, :], c.rowno[:, 0:1], None, ALU.is_equal).then_inc(step, 1)
            nc.vector.tensor_scalar(c.lower[:, :], c.iota[:, :], c.rowno[:, 0:1], None, ALU.is_gt).then_inc(step, 1)
            nc.vector.tensor_scalar(c.valid[:, :], c.rowno[:, :], float(LAST), None, ALU.is_lt).then_inc(step, 1)
            dve.wait_ge(step, 1)
            nc.vector.tensor_copy(c.identb[:, :], c.ident[:, :]).then_inc(step, 1)


class Edges:

    def __init__(self, c, name, typed):
        self.node = c.keep(f"{name}_node", [P, CH], i32)
        self.local = c.keep(f"{name}_local", [P, CH], fp32)
        self.block = c.keep(f"{name}_block", [1, UP * P], i32)
        if typed:
            self.row = c.keep(f"{name}_row", [P, CH], i32)
            self.relation = c.keep(f"{name}_relation", [P, CH], fp32)
            self.weight = c.keep(f"{name}_weight", [P, CH], fp32)


class Sort:

    def __init__(self, c, name, key, other, relation, listed, owners, owner, dest, rec):
        self.c, self.name, self.key, self.other, self.relation = c, name, key, other, relation
        self.listed, self.owners, self.owner, self.dest, self.rec = listed, owners, owner, dest, rec
        self.words = 4 if relation is not None else 2

    def place(self, work):
        c, nc, name = self.c, self.c.nc, self.name
        keyb, keyf, eq, cum, pos = work
        dest, rec = self.dest, self.rec
        loads = 3 if self.relation is not None else 2
        before_bank, all_bank = (0, 1) if self.relation is not None else (2, 3)
        before, overall = c.bank[before_bank][:, 0:KEYS], c.bank[all_bank][:, 0:KEYS]
        with c.scope() as sb:
            keyv = sb(f"{name}_key", [P, EC], i32)
            othv = sb(f"{name}_other", [P, EC], i32)
            relv = sb(f"{name}_relation", [P, EC], i32) if self.relation is not None else None
            total = sb(f"{name}_total", [P, KEYS], fp32)
            units = sb(f"{name}_units", [P, KEYS], fp32)
            uniti = sb(f"{name}_uniti", [P, KEYS], i32)
            upto = sb(f"{name}_upto", [P, KEYS], fp32)
            first = sb(f"{name}_first", [P, KEYS], fp32)
            start = sb(f"{name}_start", [P, KEYS], fp32)
            zero = sb(f"{name}_zero", [P, KEYS], fp32)
            owner = sb(f"{name}_ownerf", [P, UP], fp32)
            blank = sb(f"{name}_blank", [P, CH // 16, self.words], i32)
            with c.stage(name, "filled", "loaded", "blanked", "step", "totalled", "summed", "placing") as (
                    block, filled, loaded, blanked, step, totalled, summed, placing):

                @block.gpsimd
                def _(pool):
                    nc.gpsimd.memset(keyv[:, :], PADNODE).then_inc(filled, 1)
                    nc.gpsimd.memset(othv[:, :], 0).then_inc(filled, 1)
                    if relv is not None:
                        nc.gpsimd.memset(relv[:, :], 0).then_inc(filled, 1)
                    nc.gpsimd.memset(blank[:, :, :], 0).then_inc(filled, 1)
                    pool.wait_ge(filled, loads + 1)
                    nc.gpsimd.memset(blank[:, :, 1:2], -1).then_inc(filled, 1)

                @block.sync
                def _(sp):
                    sp.wait_ge(filled, loads + 2)
                    for dst_sb, src_dram in ((keyv, self.key), (othv, self.other), (relv, self.relation)):
                        if dst_sb is not None:
                            sp.dma_start(dst_sb[0:P - 1, :],
                                         src_dram[0:(P - 1) * EC].rearrange("(p c) -> p c", c=EC)).then_inc(loaded, 16)
                            sp.dma_start(dst_sb[P - 1:P, 0:ETAIL],
                                         src_dram[(P - 1) * EC:E].rearrange("(p c) -> p c", p=1)).then_inc(loaded, 16)
                    w = CH // 16 * self.words
                    for k in range(16):
                        sp.dma_start(self.listed[:, k * w:(k + 1) * w],
                                     blank[:, :, :].rearrange("p c w -> p (c w)")).then_inc(blanked, 16)
                    sp.wait_ge(blanked, 16 * 16)

                @block.vector
                def _(dve):
                    o = Order(dve, step)
                    o.link(nc.vector.memset(zero[:, :], 0.0))
                    o.link(nc.vector.memset(pos[:, :], 0.0))
                    dve.wait_ge(loaded, 32 * loads)
                    o.link(nc.vector.tensor_scalar(keyb[:, :], keyv[:, :], 7, None, ALU.logical_shift_right))
                    o.link(nc.vector.tensor_copy(keyf[:, :], keyb[:, :]))

                    def count(k):
                        ck = Order(dve, totalled, k)
                        ck.link(nc.vector.tensor_scalar(cum[:, :], keyf[:, :], c.keyno[:, bass.ds(k, 1)], 0.0,
                                                        ALU.is_equal, ALU.add, accum_out=total[:, bass.ds(k, 1)]))

                    rounds(dve, KEYS, count)
                    dve.wait_ge(summed, 1)
                    o.link(nc.vector.tensor_scalar(uniti[:, :], overall, float(UNIT * P - 1), None, ALU.add))
                    o.link(nc.vector.tensor_scalar(uniti[:, :], uniti[:, :], USHIFT, None, ALU.logical_shift_right))
                    o.link(nc.vector.tensor_copy(units[:, :], uniti[:, :]))
                    o.link(nc.vector.tensor_tensor_scan(upto[:, :], units[:, :], zero[:, :], 0.0, ALU.add, ALU.add))
                    o.link(nc.vector.tensor_tensor(first[:, :], upto[:, :], units[:, :], ALU.subtract))
                    o.link(nc.vector.tensor_scalar(start[:, :], first[:, :], float(UNIT * P), -1.0, ALU.mult, ALU.add))
                    o.link(nc.vector.tensor_tensor(start[:, :], start[:, :], before, ALU.add))
                    o.link(nc.vector.memset(owner[:, :], 0.0))
                    for k in range(1, KEYS):
                        o.link(nc.vector.scalar_tensor_tensor(owner[:, :], c.unitno[:, :], first[:, k:k + 1],
                                                              owner[:, :], ALU.is_ge, ALU.add))
                    o.link(nc.vector.tensor_copy(self.owner[:, :], owner[:, :]))

                    def place(k):
                        pk = Order(dve, placing, k * 4)
                        pk.link(nc.vector.tensor_scalar(eq[:, :], keyf[:, :], c.keyno[:, bass.ds(k, 1)], None,
                                                        ALU.is_equal))
                        pk.link(nc.vector.tensor_tensor_scan(cum[:, :], eq[:, :], eq[:, :], start[:, bass.ds(k, 1)],
                                                             ALU.add, ALU.bypass))
                        pk.link(nc.vector.tensor_tensor(cum[:, :], cum[:, :], eq[:, :], ALU.mult))
                        pk.link(nc.vector.tensor_tensor(pos[:, :], pos[:, :], cum[:, :], ALU.add))

                    rounds(dve, KEYS, place)
                    o.link(nc.vector.tensor_copy(dest[:, :], pos[:, :]))
                    o.link(nc.vector.tensor_scalar(keyb[:, :], dest[:, :], 7, None, ALU.logical_shift_right))
                    o.link(nc.vector.tensor_scalar(dest[:, :], dest[:, :], P - 1, None, ALU.bitwise_and))
                    o.link(nc.vector.scalar_tensor_tensor(dest[:, :], dest[:, :], float(CH), keyb[:, :], ALU.mult,
                                                          ALU.add))
                    o.link(nc.vector.tensor_copy(rec[:, :, 0], othv[:, :]))
                    o.link(nc.vector.tensor_scalar(rec[:, :, 1], keyv[:, :], P - 1, None, ALU.bitwise_and))
                    if relv is not None:
                        o.link(nc.vector.scalar_tensor_tensor(rec[:, :, 2], othv[:, :], float(R), relv[:, :], ALU.mult,
                                                              ALU.add))
                        o.link(nc.vector.tensor_copy(rec[:, :, 3], relv[:, :]))
                    else:
                        o.link(nc.vector.tensor_tensor(cum[:, :], keyv[:, :], othv[:, :], ALU.not_equal))
                        o.link(nc.vector.scalar_tensor_tensor(keyf[:, :], rec[:, :, 1], 1.0, cum[:, :], ALU.add,
                                                              ALU.mult))
                        o.link(nc.vector.tensor_scalar(rec[:, :, 1], keyf[:, :], -1.0, None, ALU.add))
                    self.placed, self.placed_at = step, o.n

                self.blanked = blanked

                @block.tensor
                def _(pe):
                    pe.wait_ge(totalled, KEYS)
                    nc.tensor.matmul(before, c.lower[:, :], total[:, :], start=True, stop=True)
                    nc.tensor.matmul(overall, c.ones[:, :], total[:, :], start=True, stop=True).then_inc(summed, 1)

    def scatter(self, inside):
        c, nc, name = self.c, self.c.nc, self.name
        rows = self.listed.rearrange("p (c w) -> (p c) w", w=self.words)
        with c.scope() as sb:
            ib = sb(f"{name}_scatter_index", [P, 2, SC], i32)
            rb = sb(f"{name}_scatter_rows", [P, 2, SC, self.words], i32)
            with c.stage(f"{name}send", "copied", "sent0", "sent1", "started") as (block, copied, sent0, sent1, started):
                sent = (sent0, sent1)

                @block.gpsimd
                def _(pool):
                    if inside:
                        pool.wait_ge(self.placed, self.placed_at)
                        pool.wait_ge(self.blanked, 16 * 16)

                    def some(i):
                        for h in range(2):
                            col = i * (2 * SC) + h * SC
                            if later(i):
                                pool.wait_ge(sent[h], i * (16 * SC))
                            nc.gpsimd.tensor_copy(ib[:, h, :], self.dest[:, bass.ds(col, SC)]).then_inc(copied, 1)
                            nc.gpsimd.tensor_copy(rb[:, h, :, :], self.rec[:, bass.ds(col, SC), :]).then_inc(copied, 1)
                            pool.wait_ge(copied, i * 4 + (2 * h + 2))
                            pool.sem_inc(started, 1)
                            for k in range(SC):
                                nc.gpsimd.indirect_dma_start(
                                    rows, bass.IndirectOffsetOnAxis(ap=ib[:, h, k:k + 1], axis=0),
                                    rb[:, h, k, :], None).then_inc(sent[h], 16)

                    rounds(pool, EC // (2 * SC), some)
                    for h in range(2):
                        pool.wait_ge(sent[h], 16 * SC * (EC // (2 * SC)))

    def read(self, out):
        c, nc, name = self.c, self.c.nc, self.name
        with c.scope() as sb:
            got = sb(f"{name}_list", [P, CH, self.words], i32)
            with c.stage(f"{name}read", "back", "ownerout", "ownerin", "step") as (block, back, ownerout, ownerin, step):
                @block.sync
                def _(sp):
                    sp.dma_start(got[:, :, :].rearrange("p c w -> p (c w)"), self.listed).then_inc(back, 16)
                    sp.dma_start(self.owners.rearrange("(p c) -> p c", p=P), self.owner[:, :]).then_inc(ownerout, 16)
                    sp.wait_ge(ownerout, 16)
                    sp.dma_start(out.block[0:1, :], self.owners.rearrange("(a c) -> a c", a=1)).then_inc(ownerin, 16)
                    sp.wait_ge(ownerin, 16)

                @block.vector
                def _(dve):
                    dve.wait_ge(back, 16)
                    dve.wait_ge(ownerin, 16)
                    o = Order(dve, step)
                    o.link(nc.vector.tensor_copy(out.node[:, :], got[:, :, 0]))
                    o.link(nc.vector.tensor_copy(out.local[:, :], got[:, :, 1]))
                    if self.words == 4:
                        o.link(nc.vector.tensor_copy(out.row[:, :], got[:, :, 2]))
                        o.link(nc.vector.tensor_copy(out.relation[:, :], got[:, :, 3]))


def unit_blocks(nc, which, row, g):
    return nc.values_load_multi_w_load_instructions(row[0:1, bass.ds(g * GU, GU)], engines=(which,), min_val=0,
                                                    max_val=KEYS - 1)[1]


def same(iota, n, w=P):
    return iota[:, 0:w].rearrange("p (a w) -> p a w", a=1).to_broadcast([P, n, w])


def per_chunk(values, at, w):
    return values[:, bass.ds(at, GRP)].rearrange("p (k a) -> p k a", a=1).to_broadcast([P, GRP, w])


def pipeline(eng, step, drain=None):
    def both(i):
        step(i, 0, i, 1)
        step(i, 1, i + 1, 0)

    rounds(eng, PAIRS - 1, both)
    step(PAIRS - 1, 0, PAIRS - 1, 1)
    step(PAIRS - 1, 1, None, None)
    if drain:
        drain(PAIRS - 1, 1)


def two_ahead(eng, step):
    def both(i):
        step(i, 0, i + 1)
        step(i, 1, i + 1)

    rounds(eng, PAIRS - 1, both)
    step(PAIRS - 1, 0, None)
    step(PAIRS - 1, 1, None)


def before(i, h):
    return (i, 0) if h else (i - 1, 1)


def gather_groups(nc, pool, table, idx, ib, G, gathered, free, copied, started):
    def one(i):
        for h in range(2):
            if later(i):
                for sem, rise in free[h]:
                    pool.wait_ge(sem, i * rise)
            nc.gpsimd.tensor_copy(ib[:, h, :], idx[:, bass.ds(i * (2 * GRP) + h * GRP, GRP)]).then_inc(copied, 1)
            pool.wait_ge(copied, i * 2 + (h + 1))
            pool.sem_inc(started, 1)
            for k in range(GRP):
                nc.gpsimd.indirect_dma_start(G[:, h, k, :], None, table,
                                             bass.IndirectOffsetOnAxis(ap=ib[:, h, k:k + 1], axis=0)
                                             ).then_inc(gathered[h], 16)

    rounds(pool, PAIRS, one)
    for h in range(2):
        pool.wait_ge(gathered[h], 16 * GRP * PAIRS)


def edge_pass(c, name, table, idx, edges, acc, weighted=False):
    nc = c.nc
    width = table.shape[-1]
    with (c.scope() as sb,
          c.stage(name, "gathered0", "gathered1", "used0", "used1", "copied", "started", "marked0", "marked1",
                  "weighed0", "weighed1", "added") as (
                      block, gathered0, gathered1, used0, used1, copied, started, marked0, marked1,
                      weighed0, weighed1, added)):
        gathered, used, marked, weighed = (gathered0, gathered1), (used0, used1), (marked0, marked1), (weighed0, weighed1)
        G = sb(f"{name}_G", [P, 2, GRP, width], fp32)
        onehot = sb(f"{name}_onehot", [P, 2, GRP, P], fp32)
        ib = sb(f"{name}_ib", [P, 2, GRP], i32)
        rows = sb(f"{name}_rows", [P, 2, GRP, width], fp32) if weighted else G

        @block.gpsimd
        def _(pool):
            gather_groups(nc, pool, table, idx, ib, G, gathered,
                          [[((weighed if weighted else used)[h], 1)] for h in range(2)], copied, started)

        @block.vector
        def _(dve):
            def mark(i, h):
                if later(i):
                    dve.wait_ge(used[h], i)
                nc.vector.tensor_tensor(onehot[:, h, :, :], same(c.iota, GRP),
                                        per_chunk(edges.local, i * (2 * GRP) + h * GRP, P),
                                        ALU.is_equal).then_inc(marked[h], 1)

            def weigh(i, h):
                dve.wait_ge(gathered[h], i * (16 * GRP) + 16 * GRP)
                nc.vector.tensor_tensor(rows[:, h, :, :], G[:, h, :, :],
                                        per_chunk(edges.weight, i * (2 * GRP) + h * GRP, width),
                                        ALU.mult).then_inc(weighed[h], 1)

            def add(i, h):
                b = unit_blocks(nc, dve.engine, edges.block, i * 2 + h)
                dve.wait_ge(used[h], i + 1)
                o = Order(dve, added, i * (2 * GU) + h * GU)
                for u in range(GU):
                    at = acc[:, bass.ds(b[u], 1), :]
                    o.link(nc.vector.tensor_tensor(at, at, c.bank[h][:, u * width:(u + 1) * width].rearrange(
                        "p (a w) -> p a w", a=1), ALU.add))

            def step(i, h, ni, nh):
                if ni is not None:
                    mark(ni, nh)
                if later(i) or h:
                    add(*before(i, h))
                if weighted:
                    weigh(i, h)

            mark(0, 0)
            pipeline(dve, step, add)

        @block.tensor
        def _(pe):
            def products(i):
                for h in range(2):
                    pe.wait_ge(marked[h], i + 1)
                    if weighted:
                        pe.wait_ge(weighed[h], i + 1)
                    else:
                        pe.wait_ge(gathered[h], i * (16 * GRP) + 16 * GRP)
                    if later(i):
                        pe.wait_ge(added, i * (2 * GU) - GU + h * GU)
                    for k in range(GRP):
                        u = k // UNIT
                        last = nc.tensor.matmul(c.bank[h][:, u * width:(u + 1) * width], onehot[:, h, k, :],
                                                rows[:, h, k, :], start=k % UNIT == 0, stop=k % UNIT == UNIT - 1)
                    last.then_inc(used[h], 1)

            rounds(pe, PAIRS, products)


def relation_weights(c, edges, counts):
    nc = c.nc
    HB = GRP // 2
    with c.scope() as sb:
        onehot = sb("cw_onehot", [P, 2, GRP, P], bf16)
        onehotT = sb("cw_turned", [P, 2, GRP, P], fp32)
        rel = sb("cw_relation", [P, 2, GRP, R], bf16)
        picked = sb("cw_picked", [P, 2, GRP, R], fp32)

        def mark_node(i, h):
            return nc.vector.tensor_tensor(onehot[:, h, :, :], same(c.iota, GRP),
                                           per_chunk(edges.local, i * (2 * GRP) + h * GRP, P), ALU.is_equal)

        def mark_relation(i, h):
            return nc.vector.tensor_tensor(rel[:, h, :, :], same(c.iota, GRP, R),
                                           per_chunk(edges.relation, i * (2 * GRP) + h * GRP, R), ALU.is_equal)

        with c.stage("count", "used0", "used1", "marked0", "marked1", "added", "cleared") as (
                block, used0, used1, marked0, marked1, added, cleared):
            used, marked = (used0, used1), (marked0, marked1)

            @block.vector
            def _(dve):
                nc.vector.memset(counts[:, :, :], 0.0).then_inc(cleared, 1)
                dve.wait_ge(cleared, 1)

                def mark(i, h):
                    if later(i):
                        dve.wait_ge(used[h], i)
                    mark_node(i, h)
                    mark_relation(i, h).then_inc(marked[h], 1)

                def add(i, h):
                    b = unit_blocks(nc, dve.engine, edges.block, i * 2 + h)
                    dve.wait_ge(used[h], i + 1)
                    o = Order(dve, added, i * (2 * GU) + h * GU)
                    for u in range(GU):
                        at = counts[:, bass.ds(b[u], 1), :]
                        o.link(nc.vector.tensor_tensor(at, at, c.bank[h][:, u * R:(u + 1) * R].rearrange(
                            "p (a w) -> p a w", a=1), ALU.add))

                def step(i, h, ni, nh):
                    if ni is not None:
                        mark(ni, nh)
                    add(i, h)

                mark(0, 0)
                pipeline(dve, step)

            @block.tensor
            def _(pe):
                def products(i):
                    for h in range(2):
                        pe.wait_ge(marked[h], i + 1)
                        if later(i):
                            pe.wait_ge(added, i * (2 * GU) - GU + h * GU)
                        for k in range(GRP):
                            u = k // UNIT
                            last = nc.tensor.matmul(c.bank[h][:, u * R:(u + 1) * R], onehot[:, h, k, :],
                                                    rel[:, h, k, :], start=k % UNIT == 0, stop=k % UNIT == UNIT - 1)
                        last.then_inc(used[h], 1)

                rounds(pe, PAIRS, products)
                pe.wait_ge(added, PAIRS * 2 * GU)

        with c.stage("weigh", "marked0", "marked1", "turned0", "turned1", "spread0", "spread1", "looked0",
                     "looked1", "picked") as (block, marked0, marked1, turned0, turned1, spread0, spread1,
                                              looked0, looked1, pick):
            marked, turned, spread, looked = (marked0, marked1), (turned0, turned1), (spread0, spread1), (looked0, looked1)

            @block.vector
            def _(dve):
                def mark(i, h):
                    if later(i):
                        dve.wait_ge(turned[h], i)
                    mark_node(i, h).then_inc(marked[h], 1)

                def choose(i, h):
                    dve.wait_ge(looked[h], i + 1)
                    o = Order(dve, pick, i * 6 + h * 3)
                    for q in range(2):
                        o.link(nc.vector.tensor_tensor(
                            picked[:, h, q * HB:(q + 1) * HB, :],
                            c.bank[2 + 2 * h + q][:, 0:HB * R].rearrange("p (k r) -> p k r", r=R),
                            rel[:, h, q * HB:(q + 1) * HB, :], ALU.mult))
                    o.link(nc.vector.tensor_reduce(edges.weight[:, bass.ds(i * (2 * GRP) + h * GRP, GRP)],
                                                   picked[:, h, :, :], AX.X, ALU.add))

                def step(i, h, ni):
                    if ni is not None:
                        mark(ni, h)
                    choose(i, h)
                    if ni is not None:
                        mark_relation(ni, h)

                for h in range(2):
                    mark(0, h)
                    mark_relation(0, h)
                two_ahead(dve, step)
                o = Order(dve, pick, 6 * PAIRS)
                o.link(nc.vector.tensor_scalar(edges.weight[:, :], edges.weight[:, :], 1.0, None, ALU.max))
                nc.vector.reciprocal(edges.weight[:, :], edges.weight[:, :]).then_inc(pick, 1)

            @block.scalar
            def _(act):
                def spread_out(i):
                    for h in range(2):
                        act.wait_ge(turned[h], i + 1)
                        if later(i):
                            act.wait_ge(looked[h], i)
                        nc.scalar.activation(onehotT[:, h, :, :].rearrange("p k n -> p (k n)"),
                                             c.bank[6 + h][:, :].bitcast(bf16), ACT.Copy).then_inc(spread[h], 1)

                rounds(act, PAIRS, spread_out)

            @block.tensor
            def _(pe):
                def turn(i, h):
                    pe.wait_ge(marked[h], i + 1)
                    if later(i):
                        pe.wait_ge(spread[h], i)
                    for k in range(GRP):
                        last = nc.tensor.transpose(c.bank[6 + h][:, :].bitcast(bf16)[:, k * P:(k + 1) * P],
                                                   onehot[:, h, k, :], c.identb[:, :])
                    last.then_inc(turned[h], 1)

                def look(i, h):
                    b = unit_blocks(nc, pe.engine, edges.block, i * 2 + h)
                    pe.wait_ge(spread[h], i + 1)
                    if later(i):
                        pe.wait_ge(pick, i * 6 - 3 + h * 3)
                    for k in range(GRP):
                        at = (k % HB) * R
                        last = nc.tensor.matmul(c.bank[2 + 2 * h + k // HB][:, at:at + R], onehotT[:, h, k, :],
                                                counts[:, bass.ds(b[k // UNIT], 1), :].rearrange("p a r -> p (a r)"),
                                                start=True, stop=True)
                    last.then_inc(looked[h], 1)

                def step(i, h, ni):
                    look(i, h)
                    if ni is not None:
                        turn(ni, h)

                turn(0, 0)
                turn(0, 1)
                two_ahead(pe, step)
                pe.wait_ge(pick, PAIRS * 6)


def block_rounds(eng, one):
    def both(i):
        one(i, 0)
        one(i, 1)

    rounds(eng, NB // 2, both)
    if NB % 2:
        one(NB // 2, 0)


def node_product(c, name, src, weight, out):
    nc = c.nc
    K, M = src.shape[-1], weight.shape[-1]
    with (nc.sbuf_tensor(f"{name}_x", [P, 2, P], fp32) as xb,
          nc.sbuf_tensor(f"{name}_xT", [K, 2, P], fp32) as xT,
          c.stage(name, "blanked", "taken0", "taken1", "turned0", "turned1", "lifted0", "lifted1", "made0", "made1",
                  "out0", "out1") as (block, blanked, taken0, taken1, turned0, turned1, lifted0, lifted1,
                                      made0, made1, out0, out1)):
        taken, turned, lifted = (taken0, taken1), (turned0, turned1), (lifted0, lifted1)
        made, stored = (made0, made1), (out0, out1)

        @block.gpsimd
        def _(pool):
            nc.gpsimd.memset(xb[:, :, :], 0.0).then_inc(blanked, 1)

        @block.scalar
        def _(act):
            def take(i, h):
                if later(i):
                    act.wait_ge(turned[h], i)
                nc.scalar.activation(xb[:, h, 0:K], src[:, bass.ds(i * 2 + h, 1), :].rearrange("p a k -> p (a k)"),
                                     ACT.Copy).then_inc(taken[h], 1)

            act.wait_ge(blanked, 1)
            block_rounds(act, take)

        @block.vector
        def _(dve):
            def lift(i, h):
                dve.wait_ge(turned[h], i + 1)
                if later(i):
                    dve.wait_ge(made[h], i)
                nc.vector.tensor_copy(xT[:, h, :], c.bank[h][0:K, 0:P]).then_inc(lifted[h], 1)

            def store(i, h):
                dve.wait_ge(made[h], i + 1)
                nc.vector.tensor_copy(out[:, bass.ds(i * 2 + h, 1), :],
                                      c.bank[2 + h][:, 0:M].rearrange("p (a m) -> p a m", a=1)).then_inc(stored[h], 1)

            def one(i, h):
                lift(i, h)
                if later(i) or h:
                    store(*before(i, h))

            block_rounds(dve, one)
            store(NB // 2, 0)

        @block.tensor
        def _(pe):
            def turn(i, h):
                pe.wait_ge(taken[h], i + 1)
                if later(i):
                    pe.wait_ge(lifted[h], i)
                nc.tensor.transpose(c.bank[h][:, 0:P], xb[:, h, :], c.ident[:, :]).then_inc(turned[h], 1)

            def product(i, h):
                pe.wait_ge(lifted[h], i + 1)
                if later(i):
                    pe.wait_ge(stored[h], i)
                nc.tensor.matmul(c.bank[2 + h][:, 0:M], xT[:, h, :], weight, start=True, stop=True).then_inc(made[h], 1)

            def one(i, h):
                turn(i, h)
                if later(i) or h:
                    product(*before(i, h))

            block_rounds(pe, one)
            product(NB // 2, 0)


PIECES = 10
PW = R * D // PIECES
assert PW * PIECES == R * D and PW <= 512
RING = PIECES // 2


def relation_table(c, name, src, weight, table):
    nc = c.nc
    with (c.scope() as sb,
          c.stage(name, "weights", "blanked", "taken0", "taken1", "turned0", "turned1", "lifted0", "lifted1", "made",
                  "even", "odd", "sent0", "sent1") as (
                      block, weights, blanked, taken0, taken1, turned0, turned1, lifted0, lifted1, made,
                      even, odd, sent0, sent1)):
        xb = sb(f"{name}_x", [P, 2, P], fp32)
        xT = sb(f"{name}_xT", [D, 2, P], fp32)
        w = sb(f"{name}_w", [D, R, D], fp32)
        y = sb(f"{name}_y", [P, 2, R * D], fp32)
        taken, turned, lifted, sent = (taken0, taken1), (turned0, turned1), (lifted0, lifted1), (sent0, sent1)
        HP = PIECES // 2
        wf = w[:, :, :].rearrange("d r k -> d (r k)")

        @block.gpsimd
        def _(pool):
            nc.gpsimd.memset(xb[:, :, :], 0.0).then_inc(blanked, 1)

        @block.sync
        def _(sp):
            sp.dma_start(w[:, :, :], weight.rearrange("r d k -> d r k")).then_inc(weights, 16)

            def send(i, h):
                sp.wait_ge(even, i * (2 * HP) + (h + 1) * HP)
                sp.wait_ge(odd, i * (2 * HP) + (h + 1) * HP)
                sp.dma_start(table[bass.ds(i * 2 * P + h * P, P), :], y[:, h, :]).then_inc(sent[h], 16)

            block_rounds(sp, send)
            sp.wait_ge(sent[0], 16 * (NB // 2 + 1))
            sp.wait_ge(sent[1], 16 * (NB // 2))

        def store_piece(eng, copy, i, h, j):
            eng.wait_ge(made, i * (2 * PIECES) + (h * PIECES + j + 1))
            if later(i) and j < 2:
                eng.wait_ge(sent[h], i * 16)
            return copy(y[:, h, j * PW:(j + 1) * PW], c.bank[2 + j % RING][:, 0:PW])

        @block.scalar
        def _(act):
            def one(i, h):
                if later(i):
                    act.wait_ge(turned[h], i)
                nc.scalar.activation(xb[:, h, 0:D], src[:, bass.ds(i * 2 + h, 1), :].rearrange("p a k -> p (a k)"),
                                     ACT.Copy).then_inc(taken[h], 1)

            def pieces(i, h):
                for j in range(1, PIECES, 2):
                    store_piece(act, lambda o, s: nc.scalar.activation(o, s, ACT.Copy), i, h, j).then_inc(odd, 1)

            def step(i, h):
                one(i, h)
                if later(i) or h:
                    pieces(*before(i, h))

            act.wait_ge(blanked, 1)
            block_rounds(act, step)
            pieces(NB // 2, 0)

        @block.vector
        def _(dve):
            def lift(i, h):
                dve.wait_ge(turned[h], i + 1)
                if later(i):
                    dve.wait_ge(made, i * (2 * PIECES) - PIECES + h * PIECES)
                nc.vector.tensor_copy(xT[:, h, :], c.bank[h][0:D, 0:P]).then_inc(lifted[h], 1)

            def pieces(i, h):
                for j in range(0, PIECES, 2):
                    store_piece(dve, nc.vector.tensor_copy, i, h, j).then_inc(even, 1)

            def step(i, h):
                lift(i, h)
                if later(i) or h:
                    pieces(*before(i, h))

            block_rounds(dve, step)
            pieces(NB // 2, 0)

        @block.tensor
        def _(pe):
            pe.wait_ge(weights, 16)

            def turn(i, h):
                pe.wait_ge(taken[h], i + 1)
                if later(i):
                    pe.wait_ge(lifted[h], i)
                nc.tensor.transpose(c.bank[h][:, 0:P], xb[:, h, :], c.ident[:, :]).then_inc(turned[h], 1)

            def products(i, h):
                pe.wait_ge(lifted[h], i + 1)
                for j in range(PIECES):
                    if later(i) or h or j >= RING:
                        ago = h * PIECES + j - RING
                        pe.wait_ge((even, odd)[ago % 2], i * (2 * HP) + ago // 2 + 1)
                    nc.tensor.matmul(c.bank[2 + j % RING][:, 0:PW], xT[:, h, :], wf[:, j * PW:(j + 1) * PW],
                                     start=True, stop=True).then_inc(made, 1)

            def step(i, h):
                turn(i, h)
                if later(i) or h:
                    products(*before(i, h))

            block_rounds(pe, step)
            products(NB // 2, 0)


def vector_steps(c, name, work):
    with c.stage(name, "step") as (block, stepped):
        @block.vector
        def _(dve):
            o = Order(dve, stepped)
            work(c.nc.vector, o.link)


def load(c, name, *pairs):
    with c.stage(name, "moved") as (block, moved):
        @block.sync
        def _(sp):
            for dst, src in pairs:
                sp.dma_start(dst, src).then_inc(moved, 16)
            sp.wait_ge(moved, 16 * len(pairs))


def over(vec, n):
    return vec.rearrange("p (a w) -> p a w", a=1).to_broadcast([P, n, vec.shape[-1]])


def inner(col, w):
    return col.rearrange("p (n a) -> p n a", a=1).to_broadcast([P, col.shape[-1], w])


def layer_norm(c, name, x, h, eps=1e-5):
    nc = c.nc
    with (nc.sbuf_tensor(f"{name}_sq", [P, NB, D], fp32) as sq,
          nc.sbuf_tensor(f"{name}_sum", [P, NB], fp32) as total,
          nc.sbuf_tensor(f"{name}_mean", [P, NB], fp32) as mean,
          nc.sbuf_tensor(f"{name}_sd", [P, NB], fp32) as sd,
          c.stage(name, "step", "var", "root") as (block, stepped, var, root)):
        @block.vector
        def _(dve):
            v = nc.vector
            o = Order(dve, stepped)
            X = x[:, 0:NB, :]
            o.link(v.tensor_tensor(X, X, h, ALU.add))
            o.link(v.tensor_reduce(total[:, :], X, AX.X, ALU.add))
            o.link(v.tensor_scalar(mean[:, :], total[:, :], 1.0 / D, None, ALU.mult))
            o.link(v.tensor_tensor(X, X, inner(mean[:, :], D), ALU.subtract))
            o.link(v.tensor_tensor(sq[:, :, :], X, X, ALU.mult))
            o.link(v.tensor_reduce(total[:, :], sq[:, :, :], AX.X, ALU.add))
            v.tensor_scalar(total[:, :], total[:, :], 1.0 / D, float(eps), ALU.mult, ALU.add).then_inc(var, 1)
            dve.wait_ge(root, 1)
            o.link(v.reciprocal(sd[:, :], sd[:, :]))
            o.link(v.tensor_tensor(X, X, inner(sd[:, :], D), ALU.mult))

        @block.scalar
        def _(act):
            act.wait_ge(var, 1)
            nc.scalar.activation(sd[:, :], total[:, :], ACT.Sqrt).then_inc(root, 1)


def gat_max(c, name, table, edges, best, asrc, spill, room):
    nc = c.nc
    G2 = 2 * GRP
    with (c.scope() as sb,
          c.stage(name, "gathered0", "gathered1", "copied", "started", "marked0", "marked1", "shifted0",
                  "shifted1", "turned0", "turned1", "maxed", "spilled0", "spilled1", "kept0", "kept1") as (
                      block, gathered0, gathered1, copied, started, marked0, marked1, shifted0, shifted1,
                      turned0, turned1, maxed, spilled0, spilled1, kept0, kept1)):
        kept = (kept0, kept1)
        gathered, marked, spilled = (gathered0, gathered1), (marked0, marked1), (spilled0, spilled1)
        shifted, turned = (shifted0, shifted1), (turned0, turned1)
        G = sb(f"{name}_G", [P, 2, GRP, GW], fp32)
        ib = sb(f"{name}_ib", [P, 2, GRP], i32)
        other = sb(f"{name}_other", [P, 2, GRP, P], bf16)
        alpha = room.rearrange("p b w -> p (b w)")[:, 0:4 * GRP * P].rearrange(
            "p (h u d k n) -> p h u d k n", h=2, u=GU, d=2, k=UNIT)
        top = sb(f"{name}_top", [P, 2, GU, 2], fp32)

        @block.gpsimd
        def _(pool):
            gather_groups(nc, pool, table, edges.node, ib, G, gathered,
                          [[(shifted[h], 1), (kept[h], 1), (spilled[h], 16)] for h in range(2)], copied, started)

        @block.sync
        def _(sp):
            def out(i):
                for h in range(2):
                    sp.wait_ge(gathered[h], i * (16 * GRP) + 16 * GRP)
                    sp.dma_start(spill[bass.ds(i * 2 + h, 1), :, :].rearrange("a p w -> p (a w)"),
                                 G[:, h, :, :].rearrange("p k w -> p (k w)")).then_inc(spilled[h], 16)

            rounds(sp, PAIRS, out)
            for h in range(2):
                sp.wait_ge(spilled[h], 16 * PAIRS)

        @block.vector
        def _(dve):
            def mark(i, h):
                if later(i):
                    dve.wait_ge(shifted[h], i)
                nc.vector.tensor_tensor(other[:, h, :, :], same(c.iota, GRP), per_chunk(edges.local, i * G2 + h * GRP, P),
                                        ALU.not_equal).then_inc(marked[h], 1)

            def reduce(i, h):
                b = unit_blocks(nc, dve.engine, edges.block, i * 2 + h)
                dve.wait_ge(turned[h], i + 1)
                o = Order(dve, maxed, i * (2 * (GU + 1)) + h * (GU + 1))
                for u in range(GU):
                    last = nc.vector.tensor_reduce(top[:, h, u, :], c.bank[4 * h + u][:, :].rearrange(
                        "p (d e) -> p d e", d=2), AX.X, ALU.max)
                o.link(last)
                for u in range(GU):
                    at = best[:, bass.ds(b[u], 1), :]
                    o.link(nc.vector.tensor_tensor(at, at, top[:, h, u:u + 1, :], ALU.max))

            def step(i, h, ni, nh):
                if ni is not None:
                    mark(ni, nh)
                dve.wait_ge(gathered[h], i * (16 * GRP) + 16 * GRP)
                nc.vector.tensor_copy(asrc[:, bass.ds(i * G2 + h * GRP, GRP), :],
                                      G[:, h, :, 2 * HW:GW]).then_inc(kept[h], 1)
                reduce(i, h)

            mark(0, 0)
            pipeline(dve, step)

        @block.scalar
        def _(act):
            def shift(i):
                for h in range(2):
                    act.wait_ge(marked[h], i + 1)
                    act.wait_ge(gathered[h], i * (16 * GRP) + 16 * GRP)
                    if later(i):
                        act.wait_ge(turned[h], i)
                    for k in range(GRP):
                        for d in range(2):
                            last = nc.scalar.activation(alpha[:, h, k // UNIT, d, k % UNIT, :], other[:, h, k, :],
                                                        ACT.Identity, scale=NEG,
                                                        bias=G[:, h, k, 2 * HW + d:2 * HW + d + 1])
                    last.then_inc(shifted[h], 1)

            rounds(act, PAIRS, shift)

        @block.tensor
        def _(pe):
            def turn(i):
                for h in range(2):
                    pe.wait_ge(shifted[h], i + 1)
                    if later(i):
                        pe.wait_ge(maxed, i * (2 * (GU + 1)) - (GU + 1) * (2 - h) + 1)
                    for u in range(GU):
                        for d in range(2):
                            for k in range(UNIT):
                                at = (d * UNIT + k) * P
                                last = nc.tensor.transpose(c.bank[4 * h + u][:, at:at + P], alpha[:, h, u, d, k, :],
                                                           c.ident[:, :])
                    last.then_inc(turned[h], 1)

            rounds(pe, PAIRS, turn)


def gat_pass(c, name, spill, edges, asrc, node, acc, room):
    nc = c.nc
    names = [n + d for n in ("loaded", "used", "marked", "turned", "spread", "looked", "ready", "exped",
                             "weighed", "lifted") for d in "01"]
    with c.scope() as sb, c.stage(name, *names, "added", "logits") as (block, *sems):
        loaded, used, marked, turned, spread, looked, ready, exped, weighed, lifted = (
            tuple(sems[2 * n:2 * n + 2]) for n in range(10))
        added, logits = sems[20:]
        room = room.rearrange("p b w -> p (b w)")
        rows, weighted, marks = 2 * GRP * GW, 4 * GRP * HW, 2 * GRP * P
        G = room[:, 0:rows].rearrange("p (h k w) -> p h k w", h=2, w=GW)
        x = room[:, rows:rows + weighted].rearrange("p (h k w) -> p h k w", h=2, k=GRP)
        onehot32 = room[:, rows + weighted:rows + weighted + marks].rearrange("p (h k n) -> p h k n", h=2, n=P)
        onehot = sb(f"{name}_onehot", [P, 2, GRP, P], bf16)
        onehotT = sb(f"{name}_onehotT", [P, 2, GRP, P], bf16)
        ofnode = sb(f"{name}_ofnode", [P, 2, GRP, 4], fp32)
        logit = sb(f"{name}_logit", [P, 2, GRP, 2], fp32)
        leaky = sb(f"{name}_leaky", [P, 2, GRP, 2], fp32)
        e = sb(f"{name}_exp", [P, 2, GRP, 2], fp32)

        def sums(h, u):
            return c.bank[2 * h + u // 2][:, (u % 2) * 2 * HW:(u % 2 + 1) * 2 * HW]

        nodeof = [c.bank[6 + h][:, 0:GRP * 12].rearrange("p (k w) -> p k w", w=12) for h in range(2)]

        def turnbank(h):
            return c.bank[4 + h][:, :].bitcast(bf16)

        @block.sync
        def _(sp):
            def bring(i):
                for h in range(2):
                    if later(i):
                        sp.wait_ge(weighed[h], i)
                    sp.dma_start(G[:, h, :, :].rearrange("p k w -> p (k w)"),
                                 spill[bass.ds(i * 2 + h, 1), :, :].rearrange("a p w -> p (a w)")
                                 ).then_inc(loaded[h], 16)

            rounds(sp, PAIRS, bring)

        @block.vector
        def _(dve):
            def mark(i, h):
                if later(i):
                    dve.wait_ge(turned[h], i)
                    dve.wait_ge(lifted[h], i)
                nc.vector.tensor_tensor(onehot[:, h, :, :], same(c.iota, GRP),
                                        per_chunk(edges.local, i * (2 * GRP) + h * GRP, P),
                                        ALU.is_equal).then_inc(marked[h], 1)

            def logit_of(i, h):
                dve.wait_ge(looked[h], i + 1)
                o = Order(dve, logits, i * 8 + h * 4)
                o.link(nc.vector.tensor_reduce(ofnode[:, h, :, :], nodeof[h].rearrange(
                    "p k (t w) -> p k w t", t=3), AX.X, ALU.add))
                o.link(nc.vector.tensor_tensor(logit[:, h, :, :], asrc[:, bass.ds(i * (2 * GRP) + h * GRP, GRP), :],
                                               ofnode[:, h, :, 0:2], ALU.add))
                o.link(nc.vector.scalar_tensor_tensor(leaky[:, h, :, :], logit[:, h, :, :], 0.2, logit[:, h, :, :],
                                                      ALU.mult, ALU.max))
                o.link(nc.vector.tensor_tensor(leaky[:, h, :, :], leaky[:, h, :, :], ofnode[:, h, :, 2:4],
                                               ALU.subtract))
                nc.vector.tensor_scalar(logit[:, h, :, :], leaky[:, h, :, :], 0.0, None, ALU.min).then_inc(ready[h], 1)

            def weigh(i, h):
                dve.wait_ge(loaded[h], i * 16 + 16)
                dve.wait_ge(exped[h], i + 1)
                if later(i):
                    dve.wait_ge(used[h], i)
                nc.vector.tensor_tensor(
                    x[:, h, :, :].rearrange("p k (d w) -> p k d w", d=2),
                    G[:, h, :, 0:2 * HW].rearrange("p k (d w) -> p k d w", d=2),
                    e[:, h, :, :].rearrange("p k (d a) -> p k d a", a=1).to_broadcast([P, GRP, 2, HW]),
                    ALU.mult).then_inc(weighed[h], 1)

            def blocks(i, h):
                return unit_blocks(nc, dve.engine, edges.block, i * 2 + h)

            def add(i, h, b):
                dve.wait_ge(used[h], i + 1)
                o = Order(dve, added, i * (2 * GU) + h * GU)
                for u in range(GU):
                    at = acc[:, bass.ds(b[u], 1), :]
                    o.link(nc.vector.tensor_tensor(at, at, sums(h, u).rearrange("p (a w) -> p a w", a=1), ALU.add))

            def step(i, h, ni):
                if later(i):
                    b = blocks(i - 1, h)
                logit_of(i, h)
                if later(i):
                    add(i - 1, h, b)
                weigh(i, h)
                if ni is not None:
                    mark(ni, h)

            mark(0, 0)
            mark(0, 1)
            two_ahead(dve, step)
            for h in range(2):
                add(PAIRS - 1, h, blocks(PAIRS - 1, h))

        @block.scalar
        def _(act):
            def spread_out(i, h):
                act.wait_ge(turned[h], i + 1)
                if later(i):
                    act.wait_ge(looked[h], i)
                nc.scalar.activation(onehotT[:, h, :, :].rearrange("p k n -> p (k n)"), turnbank(h),
                                     ACT.Copy).then_inc(spread[h], 1)

            def weigh(i, h):
                act.wait_ge(ready[h], i + 1)
                if later(i):
                    act.wait_ge(weighed[h], i)
                nc.scalar.activation(e[:, h, :, :], logit[:, h, :, :], ACT.Exp).then_inc(exped[h], 1)

            def lift(i, h):
                act.wait_ge(marked[h], i + 1)
                if later(i):
                    act.wait_ge(used[h], i)
                nc.scalar.activation(onehot32[:, h, :, :], onehot[:, h, :, :], ACT.Copy).then_inc(lifted[h], 1)

            def step(i, h, ni, nh):
                weigh(i, h)
                if ni is not None:
                    spread_out(ni, nh)
                lift(i, h)

            spread_out(0, 0)
            pipeline(act, step)

        @block.tensor
        def _(pe):
            def turn(i, h):
                pe.wait_ge(marked[h], i + 1)
                if later(i):
                    pe.wait_ge(spread[h], i)
                for k in range(GRP):
                    last = nc.tensor.transpose(turnbank(h)[:, k * P:(k + 1) * P], onehot[:, h, k, :], c.identb[:, :])
                last.then_inc(turned[h], 1)

            def look(i, h):
                b = unit_blocks(nc, pe.engine, edges.block, i * 2 + h)
                pe.wait_ge(spread[h], i + 1)
                if later(i):
                    pe.wait_ge(ready[h], i)
                for k in range(GRP):
                    last = nc.tensor.matmul(nodeof[h][:, k, :], onehotT[:, h, k, :],
                                            node[:, bass.ds(b[k // UNIT], 1), :].rearrange("p a w -> p (a w)"),
                                            start=True, stop=True)
                last.then_inc(looked[h], 1)

            def total(i, h):
                pe.wait_ge(weighed[h], i + 1)
                pe.wait_ge(lifted[h], i + 1)
                if later(i):
                    pe.wait_ge(added, i * (2 * GU) - GU + h * GU)
                for k in range(GRP):
                    last = nc.tensor.matmul(sums(h, k // UNIT), onehot32[:, h, k, :], x[:, h, k, :],
                                            start=k % UNIT == 0, stop=k % UNIT == UNIT - 1)
                last.then_inc(used[h], 1)

            def step(i, h, ni, nh):
                look(i, h)
                if ni is not None:
                    turn(ni, nh)
                if later(i) or h:
                    total(*before(i, h))

            turn(0, 0)
            pipeline(pe, step, total)


def by_node(table):
    return table.rearrange("(b p) w -> p b w", p=P)


def rgcn(c, x, edges, W, root, bias, res_W, res_b, ytab, out):
    nc = c.nc
    h = x
    for l in range(2):
        if l:
            relation_table(c, f"rtable{l}", h, W[l], ytab)
        with (nc.sbuf_tensor(f"rg_acc{l}", [P, KEYS, D], fp32) as acc,):
            vector_steps(c, f"rclear{l}", lambda v, link: link(v.memset(acc[:, :, :], 0.0)))
            edge_pass(c, f"rpass{l}", ytab.rearrange("n (r k) -> (n r) k", k=D), edges.row, edges, acc, weighted=True)
            with (nc.sbuf_tensor(f"rg_w{l}", [D, 2 * D], fp32) as w,
                  nc.sbuf_tensor(f"rg_b{l}", [P, 2 * D], fp32) as b,
                  nc.sbuf_tensor(f"rg_t{l}", [P, NB, 2 * D], fp32) as t):
                load(c, f"rload{l}", (w[:, 0:D], root[l]), (w[:, D:2 * D], res_W[l]),
                     (b[:, 0:D], bias[l:l + 1, :].to_broadcast([P, D])),
                     (b[:, D:2 * D], res_b[l:l + 1, :].to_broadcast([P, D])))
                node_product(c, f"rroot{l}", h, w[:, :], t)

                def combine(v, link):
                    link(v.tensor_tensor(t[:, :, :], t[:, :, :], over(b[:, :], NB), ALU.add))
                    link(v.tensor_tensor(t[:, :, 0:D], t[:, :, 0:D], acc[:, 0:NB, :], ALU.add))
                    link(v.tensor_scalar(t[:, :, :], t[:, :, :], 0.0, None, ALU.max))
                    link(v.tensor_tensor(out[:, :, :], t[:, :, 0:D], t[:, :, D:2 * D], ALU.add))

                vector_steps(c, f"rsum{l}", combine)
        h = out


def gin(c, x, edges, W1, b1, W2, b2, gamma, beta, xtab, out, eps=1e-5):
    nc = c.nc
    load(c, "gintab", (by_node(xtab), x[:, :, :]))
    with (nc.sbuf_tensor("gi_acc", [P, KEYS, D], fp32) as acc,
          nc.sbuf_tensor("gi_w", [D, 2 * D], fp32) as w,
          nc.sbuf_tensor("gi_v", [P, 4, D], fp32) as vec,
          nc.sbuf_tensor("gi_m", [P, 4, D], fp32) as m,
          nc.sbuf_tensor("gi_sq", [P, NB, D], fp32) as sq):
        load(c, "ginload", (w[:, 0:D], W1), (w[:, D:2 * D], W2),
             *((vec[:, n, :], a.rearrange("(a w) -> a w", a=1).to_broadcast([P, D]))
               for n, a in enumerate((b1, b2, gamma, beta))))

        def begin(v, link):
            link(v.memset(acc[:, NB:KEYS, :], 0.0))
            link(v.tensor_copy(acc[:, 0:NB, :], x[:, :, :]))

        vector_steps(c, "ginbegin", begin)
        edge_pass(c, "ginpass", xtab, edges.node, edges, acc)
        for n, src in ((0, acc), (1, out)):
            node_product(c, f"gin{n}", src, w[:, n * D:(n + 1) * D], out)

            def bias_relu(v, link):
                link(v.tensor_tensor(out[:, :, :], out[:, :, :], over(vec[:, n, :], NB), ALU.add))
                link(v.tensor_scalar(out[:, :, :], out[:, :, :], 0.0, None, ALU.max))

            vector_steps(c, f"ginrelu{n}", bias_relu)
        with c.stage("ginnorm", "step", "part", "whole", "var", "root") as (block, stepped, part, whole, var, sqrt):
            @block.vector
            def _(dve):
                v = nc.vector
                o = Order(dve, stepped)
                o.link(v.tensor_scalar(out[:, NB - 1, :], out[:, NB - 1, :], c.valid[:, 0:1], None, ALU.mult))
                v.tensor_reduce(m[:, 0, :], out[:, :, :].rearrange("p b d -> p d b"), AX.X, ALU.add).then_inc(part, 1)
                dve.wait_ge(whole, 1)
                o.link(v.tensor_scalar(m[:, 1, :], c.bank[0][:, 0:D], 1.0 / N, None, ALU.mult))
                o.link(v.tensor_tensor(out[:, :, :], out[:, :, :], over(m[:, 1, :], NB), ALU.subtract))
                o.link(v.tensor_scalar(out[:, NB - 1, :], out[:, NB - 1, :], c.valid[:, 0:1], None, ALU.mult))
                o.link(v.tensor_tensor(sq[:, :, :], out[:, :, :], out[:, :, :], ALU.mult))
                v.tensor_reduce(m[:, 2, :], sq[:, :, :].rearrange("p b d -> p d b"), AX.X, ALU.add).then_inc(part, 1)
                dve.wait_ge(whole, 2)
                v.tensor_scalar(m[:, 3, :], c.bank[1][:, 0:D], 1.0 / N, float(eps), ALU.mult, ALU.add).then_inc(var, 1)
                dve.wait_ge(sqrt, 1)
                o.link(v.reciprocal(m[:, 0, :], m[:, 0, :]))
                o.link(v.tensor_tensor(m[:, 0, :], m[:, 0, :], vec[:, 2, :], ALU.mult))
                o.link(v.tensor_tensor(out[:, :, :], out[:, :, :], over(m[:, 0, :], NB), ALU.mult))
                o.link(v.tensor_tensor(out[:, :, :], out[:, :, :], over(vec[:, 3, :], NB), ALU.add))

            @block.tensor
            def _(pe):
                for n in range(2):
                    pe.wait_ge(part, n + 1)
                    nc.tensor.matmul(c.bank[n][:, 0:D], c.ones[:, :], m[:, 2 * n, :], start=True,
                                     stop=True).then_inc(whole, 1)

            @block.scalar
            def _(act):
                act.wait_ge(var, 1)
                nc.scalar.activation(m[:, 0, :], m[:, 3, :], ACT.Sqrt).then_inc(sqrt, 1)


def gat_layer(c, name, src, W, a_s, a_d, edges, gtab, spill, acc):
    nc = c.nc
    with (nc.sbuf_tensor(f"{name}_node", [P, KEYS, 4], fp32) as node,
          nc.sbuf_tensor(f"{name}_parts", [P, KEYS, 12], bf16) as parts,
          nc.sbuf_tensor(f"{name}_alpha", [P, NB, 4], fp32) as alpha,
          nc.sbuf_tensor(f"{name}_best", [P, KEYS, 2], fp32) as best,
          nc.sbuf_tensor(f"{name}_self", [P, NB, 2], fp32) as self_e,
          nc.sbuf_tensor(f"{name}_self2", [P, NB, 2], fp32) as self_l,
          nc.sbuf_tensor(f"{name}_tab", [P, NB, GW], fp32) as tab,
          ExitStack() as own):
        with (nc.sbuf_tensor(f"{name}_w", [src.shape[-1], 2 * D], fp32) as w,
              nc.sbuf_tensor(f"{name}_a", [P, 4 * D], fp32) as av,
              nc.sbuf_tensor(f"{name}_h", [P, NB, 2 * D], fp32) as h):
            prod = acc[:, 0:NB, 0:2 * D]
            load(c, f"{name}load", (w[:, :], W),
                 *((av[:, (2 * n + d) * D:(2 * n + d + 1) * D], a[d:d + 1, :].to_broadcast([P, D]))
                   for n, a in enumerate((a_s, a_d)) for d in range(2)))
            node_product(c, f"{name}h", src, w[:, :], h)

            def prepare(v, link):
                for n in range(2):
                    link(v.tensor_tensor(prod, h[:, :, :], over(av[:, 2 * n * D:2 * (n + 1) * D], NB), ALU.mult))
                    for d in range(2):
                        link(v.tensor_reduce(alpha[:, :, 2 * n + d], prod[:, :, d * D:(d + 1) * D], AX.X, ALU.add))
                for d in range(2):
                    link(v.tensor_copy(tab[:, :, d * HW:d * HW + D], h[:, :, d * D:(d + 1) * D]))
                    link(v.memset(tab[:, :, d * HW + D:d * HW + D + 1], 1.0))
                link(v.tensor_copy(tab[:, :, 2 * HW:GW], alpha[:, :, 0:2]))
                link(v.memset(best[:, :, :], 0.0))
                link(v.tensor_copy(best[:, 0:NB, :], alpha[:, :, 0:2]))

            vector_steps(c, f"{name}prep", prepare)
        load(c, f"{name}tables", (by_node(gtab), tab[:, :, :]))
        asrc = own.enter_context(nc.sbuf_tensor(f"{name}_asrc", [P, CH, 2], fp32))
        gat_max(c, f"{name}max", gtab, edges, best, asrc, spill, acc[:, :, :])
        with c.stage(f"{name}own", "step", "ready", "exped") as (block, stepped, ready, exped):
            @block.vector
            def _(dve):
                v = nc.vector
                o = Order(dve, stepped)
                o.link(v.memset(node[:, :, :], 0.0))
                o.link(v.tensor_copy(node[:, 0:NB, 0:2], alpha[:, :, 2:4]))
                o.link(v.tensor_tensor(best[:, 0:NB, :], best[:, 0:NB, :], alpha[:, :, 2:4], ALU.add))
                o.link(v.scalar_tensor_tensor(node[:, 0:NB, 2:4], best[:, 0:NB, :], 0.2, best[:, 0:NB, :],
                                              ALU.mult, ALU.max))
                o.link(v.tensor_tensor(self_l[:, :, :], alpha[:, :, 0:2], alpha[:, :, 2:4], ALU.add))
                o.link(v.scalar_tensor_tensor(self_e[:, :, :], self_l[:, :, :], 0.2, self_l[:, :, :], ALU.mult, ALU.max))
                v.tensor_tensor(self_l[:, :, :], self_e[:, :, :], node[:, 0:NB, 2:4], ALU.subtract).then_inc(ready, 1)
                for n in range(3):
                    o.link(v.tensor_copy(parts[:, :, 4 * n:4 * n + 4], node[:, :, :]))
                    if n < 2:
                        o.link(v.tensor_tensor(node[:, :, :], node[:, :, :], parts[:, :, 4 * n:4 * n + 4], ALU.subtract))
                dve.wait_ge(exped, 1)
                o.link(v.memset(acc[:, NB:KEYS, :], 0.0))
                for d in range(2):
                    o.link(v.tensor_tensor(acc[:, 0:NB, d * HW:(d + 1) * HW], tab[:, :, d * HW:(d + 1) * HW],
                                           self_e[:, :, d:d + 1].to_broadcast([P, NB, HW]), ALU.mult))

            @block.scalar
            def _(act):
                act.wait_ge(ready, 1)
                nc.scalar.activation(self_e[:, :, :], self_l[:, :, :], ACT.Exp).then_inc(exped, 1)
        gat_pass(c, f"{name}pass", spill, edges, asrc, parts, acc, tab[:, :, :])

        def divide(v, link):
            for d in range(2):
                link(v.reciprocal(self_e[:, :, d:d + 1], acc[:, 0:NB, d * HW + D:(d + 1) * HW]))
                link(v.tensor_tensor(acc[:, 0:NB, d * HW:d * HW + D], acc[:, 0:NB, d * HW:d * HW + D],
                                     self_e[:, :, d:d + 1].to_broadcast([P, NB, D]), ALU.mult))

        vector_steps(c, f"{name}div", divide)


def gat(c, x, edges, W1, as1, ad1, b1, W2, as2, ad2, b2, gtab, spill, out):
    nc = c.nc
    with (nc.sbuf_tensor("gat_bias", [P, 3 * D], fp32) as bias,
          nc.sbuf_tensor("gat_acc", [P, KEYS, 2 * HW], fp32) as acc):
        load(c, "gatbias", (bias[:, 0:2 * D], b1.rearrange("(a w) -> a w", a=1).to_broadcast([P, 2 * D])),
             (bias[:, 2 * D:3 * D], b2.rearrange("(a w) -> a w", a=1).to_broadcast([P, D])))
        gat_layer(c, "gata", x, W1, as1, ad1, edges, gtab, spill, acc)
        with nc.sbuf_tensor("gat_h", [P, NB, 2 * D], fp32) as h:
            def concat(v, link):
                for d in range(2):
                    link(v.tensor_tensor(h[:, :, d * D:(d + 1) * D], acc[:, 0:NB, d * HW:d * HW + D],
                                         over(bias[:, d * D:(d + 1) * D], NB), ALU.add))

            vector_steps(c, "gatcat", concat)
            gat_layer(c, "gatb", h, W2, as2, ad2, edges, gtab, spill, acc)

        def mean(v, link):
            link(v.tensor_tensor(out[:, :, :], acc[:, 0:NB, 0:D], acc[:, 0:NB, HW:HW + D], ALU.add))
            link(v.tensor_scalar(out[:, :, :], out[:, :, :], 0.5, None, ALU.mult))
            link(v.tensor_tensor(out[:, :, :], out[:, :, :], over(bias[:, 2 * D:3 * D], NB), ALU.add))

        vector_steps(c, "gatmean", mean)


def sage(c, x, edges, W1_l, b1, W1_r, W2_l, b2, W2_r, invdeg, xtab, out):
    nc = c.nc
    with (nc.sbuf_tensor("sg_acc", [P, KEYS, D], fp32) as acc,
          nc.sbuf_tensor("sg_w1", [2 * D, 2 * D], fp32) as w1,
          nc.sbuf_tensor("sg_w2", [2 * D, 2 * D], fp32) as w2,
          nc.sbuf_tensor("sg_b", [P, 3 * D], fp32) as b,
          nc.sbuf_tensor("sg_in", [P, NB, 2 * D], fp32) as both,
          nc.sbuf_tensor("sg_h", [P, NB, 2 * D], fp32) as h):
        load(c, "sageload", (by_node(xtab), x[:, :, :]), (w1[0:D, :], W1_l), (w1[D:2 * D, :], W1_r),
             (w2[:, 0:D], W2_l), (w2[:, D:2 * D], W2_r),
             (b[:, 0:2 * D], b1.rearrange("(a w) -> a w", a=1).to_broadcast([P, 2 * D])),
             (b[:, 2 * D:3 * D], b2.rearrange("(a w) -> a w", a=1).to_broadcast([P, D])))
        vector_steps(c, "sageclear0", lambda v, link: link(v.memset(acc[:, :, :], 0.0)))
        edge_pass(c, "sagepass0", xtab, edges.node, edges, acc)

        def mean_and_own(v, link):
            link(v.tensor_tensor(both[:, :, 0:D], acc[:, 0:NB, :], inner(invdeg[:, :], D), ALU.mult))
            link(v.tensor_copy(both[:, :, D:2 * D], x[:, :, :]))

        vector_steps(c, "sagemean", mean_and_own)
        node_product(c, "sage0", both, w1[:, :], h)

        def relu(v, link):
            link(v.tensor_tensor(h[:, :, :], h[:, :, :], over(b[:, 0:2 * D], NB), ALU.add))
            link(v.tensor_scalar(h[:, :, :], h[:, :, :], 0.0, None, ALU.max))

        vector_steps(c, "sagerelu", relu)
        node_product(c, "sage1", h, w2[:, :], both)
        load(c, "sagetab", (by_node(xtab), both[:, :, 0:D]))
        vector_steps(c, "sageclear1", lambda v, link: link(v.memset(acc[:, :, :], 0.0)))
        edge_pass(c, "sagepass1", xtab, edges.node, edges, acc)

        def total(v, link):
            link(v.tensor_tensor(out[:, :, :], acc[:, 0:NB, :], inner(invdeg[:, :], D), ALU.mult))
            link(v.tensor_tensor(out[:, :, :], out[:, :, :], both[:, :, D:2 * D], ALU.add))
            link(v.tensor_tensor(out[:, :, :], out[:, :, :], over(b[:, 2 * D:3 * D], NB), ALU.add))

        vector_steps(c, "sagesum", total)


def program(nc, x, src, dst, relation, L0_W, L0_root, L0_bias, L0_res_W, L0_res_b, L1_W1, L1_b1, L1_W2, L1_b2,
            L1_gamma, L1_beta, L2_W1, L2_as1, L2_ad1, L2_b1, L2_W2, L2_as2, L2_ad2, L2_b2, L3_W1_l, L3_b1,
            L3_W1_r, L3_W2_l, L3_b2, L3_W2_r, out):
    ctx = ExitStack()
    with ctx:
        def dram(name, shape, dt):
            return nc.dram_tensor(name, shape, dt, kind="Internal").ap()

        c = Chip(nc, ctx)
        by_dst = dram("edges_by_dst", [P, CH * 4], i32)
        by_src = dram("edges_by_src", [P, CH * 2], i32)
        dst_owners = dram("dst_unit_blocks", [UP * P], i32)
        src_owners = dram("src_unit_blocks", [UP * P], i32)
        ytab = dram("relation_products", [NB * P, R * D], fp32)
        xtab = dram("node_rows", [NB * P, D], fp32)
        gtab = dram("gat_rows", [NB * P, GW], fp32)
        spill = dram("gat_edge_rows", [2 * PAIRS, P, GRP * GW], fp32)
        constants(c)
        X = c.keep("x", [P, NB, D], fp32)
        invdeg = c.keep("invdeg", [P, NB], fp32)
        owner_dst = c.keep("owner_dst", [P, UP], i32)
        owner_src = c.keep("owner_src", [P, UP], i32)
        later_use = c.keep("places_or_h", [P, 3 * EC], i32)
        H = later_use[:, 0:NB * D].bitcast(fp32).rearrange("p (b d) -> p b d", d=D)
        vector_steps(c, "padrows", lambda v, link: link(v.memset(X[:, NB - 1, :], 0.0)))
        load(c, "loadx", (X[:, 0:NB - 1, :], x[0:(NB - 1) * P, :].rearrange("(b p) d -> p b d", p=P)),
             (X[0:LAST, NB - 1, :], x[(NB - 1) * P:N, :]))
        sort_src = Sort(c, "sorts", src, dst, None, by_src, src_owners, owner_src, later_use[:, 0:EC],
                        later_use[:, EC:3 * EC].rearrange("p (c w) -> p c w", w=2))
        with ExitStack() as tmp:
            def sb(n, shape, dt):
                return tmp.enter_context(nc.sbuf_tensor(f"sort_{n}", shape, dt))

            sort_dst = Sort(c, "sortd", dst, src, relation, by_dst, dst_owners, owner_dst,
                            sb("dest", [P, EC], i32)[:, :], sb("records", [P, EC, 4], i32)[:, :, :])
            work = [sb(n, [P, EC], dt) for n, dt in (
                ("keyblock", i32), ("keyblockf", fp32), ("is_key", fp32), ("running", fp32), ("slot", fp32))]
            with c.together():
                sort_dst.place(work)
                sort_src.place(work)
                relation_table(c, "rtable0", X, L0_W[0], ytab)
                sort_dst.scatter(True)
        to_dst = Edges(c, "to_dst", typed=True)
        to_src = Edges(c, "to_src", typed=False)
        with nc.sbuf_tensor("counts", [P, KEYS, R], fp32) as counts:
            with c.together():
                sort_src.scatter(False)
                sort_dst.read(to_dst)
                relation_weights(c, to_dst, counts)

            def degrees(v, link):
                link(v.tensor_reduce(invdeg[:, :], counts[:, 0:NB, :], AX.X, ALU.add))
                link(v.tensor_scalar(invdeg[:, :], invdeg[:, :], 1.0, None, ALU.max))
                link(v.reciprocal(invdeg[:, :], invdeg[:, :]))

            vector_steps(c, "degrees", degrees)
        sort_src.read(to_src)
        rgcn(c, X, to_dst, L0_W, L0_root, L0_bias, L0_res_W, L0_res_b, ytab, H)
        layer_norm(c, "norm0", X, H[:, :, :])
        gin(c, X, to_src, L1_W1, L1_b1, L1_W2, L1_b2, L1_gamma, L1_beta, xtab, H)
        layer_norm(c, "norm1", X, H[:, :, :])
        gat(c, X, to_dst, L2_W1, L2_as1, L2_ad1, L2_b1, L2_W2, L2_as2, L2_ad2, L2_b2, gtab, spill, H)
        layer_norm(c, "norm2", X, H[:, :, :])
        sage(c, X, to_dst, L3_W1_l, L3_b1, L3_W1_r, L3_W2_l, L3_b2, L3_W2_r, invdeg, xtab, H)
        layer_norm(c, "norm3", X, H[:, :, :])
        load(c, "store", (out[0:(NB - 1) * P, :].rearrange("(b p) d -> p b d", p=P), X[:, 0:NB - 1, :]),
             (out[(NB - 1) * P:N, :], X[0:LAST, NB - 1, :]))


INPUTS = ["x", "src", "dst", "edge_type_65", "L0_gnn_W", "L0_gnn_root", "L0_gnn_bias", "L0_gnn_res_W",
          "L0_gnn_res_b", "L1_gnn_W1", "L1_gnn_b1", "L1_gnn_W2", "L1_gnn_b2", "L1_gnn_gamma", "L1_gnn_beta",
          "L2_gnn_W1", "L2_gnn_as1", "L2_gnn_ad1", "L2_gnn_b1", "L2_gnn_W2", "L2_gnn_as2", "L2_gnn_ad2",
          "L2_gnn_b2", "L3_gnn_W1_l", "L3_gnn_b1", "L3_gnn_W1_r", "L3_gnn_W2_l", "L3_gnn_b2", "L3_gnn_W2_r"]


def kernel(**inputs):
    import numpy as np
    import concourse.bacc as bacc
    from concourse import mybir as mb
    from concourse.bass_utils import run_bass_kernel_spmd

    nc = bacc.Bacc("TRN2", target_bir_lowering=False, num_devices=1)
    arrays, args = {}, []
    for name in INPUTS:
        a = np.ascontiguousarray(inputs[name])
        arrays[f"in_{name}"] = a
        args.append(nc.dram_tensor(f"in_{name}", a.shape, mb.dt.from_np(a.dtype), kind="ExternalInput").ap())
    args.append(nc.dram_tensor("out_x", (N, D), mb.dt.float32, kind="ExternalOutput").ap())
    program(nc, *args)
    r = run_bass_kernel_spmd(nc, [arrays], core_ids=[0])
    return r.results[0]["out_x"]
```
